# Optimizing a Trainium2 kernel written in Bass

```python
import numpy as np
import jax
import jax.numpy as jnp

def _softmax(x, axis=-1):
    return jax.nn.softmax(x, axis=axis)

def _gelu(x):
    return jax.nn.gelu(x, approximate=True)

def _silu(x):
    return jax.nn.silu(x)

def _sigmoid(x):
    return jax.nn.sigmoid(x)

def _layernorm(x, axis=-1, eps=1e-05):
    m = jnp.mean(x, axis=axis, keepdims=True)
    v = jnp.var(x, axis=axis, keepdims=True)
    return (x - m) / jnp.sqrt(v + eps)

def _scatter_add(tgt, idx, src, axis=0):
    return tgt.at[idx].add(src)

def _segment_sum(src, seg, n):
    return jax.ops.segment_sum(src, seg, n)
kernel_name = 'mk_gnn_preln_d4_gnn_r16_f4b2e1'

def setup_inputs(seed: int=0):
    np.random.seed(seed)
    _w = jnp.asarray

    def _rec_inputs():
        import jax
        import jax.numpy as jnp
        _gk = jax.random.key(seed)
        x = -0.0003713 + 1 * jax.random.normal(jax.random.fold_in(_gk, 1), (6250, 128), jnp.float32)
        src = jax.random.randint(jax.random.fold_in(_gk, 2), (200000,), 0, 6250, jnp.int32)
        dst = jnp.minimum((6250 * jax.random.uniform(jax.random.fold_in(_gk, 3), (200000,)) ** 2.0).astype(jnp.int32), 99999)
        _o = jnp.argsort(dst, stable=True)
        src = src[_o]
        dst = dst[_o]
        edge_attr_16 = -5.3897e-05 + 0.999841 * jax.random.normal(jax.random.fold_in(_gk, 12), (200000, 16), jnp.float32)
        edge_type_8 = jax.random.randint(jax.random.fold_in(_gk, 14), (200000,), 0, 8, jnp.int32)
        return (x, src, dst, edge_attr_16, edge_type_8)
    x, src, dst, edge_attr_16, edge_type_8 = _rec_inputs()

    def _L0_gnn_setup():
        import jax, jax.numpy as jnp
        import numpy as np
        N_NODES = 6250
        N_EDGES = 100000
        D_IN = 128
        D_OUT = 128
        key = jax.random.key(seed)
        k1, k2, k3, k4 = jax.random.split(key, 4)
        x = jax.random.normal(k1, (N_NODES, D_IN), dtype=jnp.float32)
        edge_index = jax.random.randint(k2, (2, N_EDGES), 0, N_NODES, dtype=jnp.int64)
        s = 1.0 / np.sqrt(D_IN)
        W_l = jax.random.uniform(k3, (D_OUT, D_IN), jnp.float32, -s, s)
        b_l = jnp.zeros((D_OUT,), jnp.float32)
        W_r = jax.random.uniform(k4, (D_OUT, D_IN), jnp.float32, -s, s)
        return {'x': x, 'edge_index': edge_index, 'W_l': W_l, 'b_l': b_l, 'W_r': W_r}
    _L0_gnn_all = _L0_gnn_setup()
    _L0_gnn_in = {k: v for k, v in _L0_gnn_all.items() if k in ('W_l', 'b_l', 'W_r')}
    del _L0_gnn_all

    def _L1_gnn_setup():
        import jax, jax.numpy as jnp
        import numpy as np
        N_NODES = 6250
        N_EDGES = 100000
        IN_FEAT = 128
        OUT_FEAT = 128
        NUM_RELS = 8
        NUM_BASES = 2
        key = jax.random.key(seed)
        ks = jax.random.split(key, 8)
        feat = jax.random.normal(ks[0], (N_NODES, IN_FEAT), dtype=jnp.float32)
        edge_src = jax.random.randint(ks[1], (N_EDGES,), 0, N_NODES, dtype=jnp.int32)
        edge_dst = jnp.sort(jax.random.randint(ks[2], (N_EDGES,), 0, N_NODES, dtype=jnp.int32))
        etypes = jax.random.randint(ks[3], (N_EDGES,), 0, NUM_RELS, dtype=jnp.int32)
        bound = 1.0 / np.sqrt(IN_FEAT)
        W = jax.random.uniform(ks[4], (NUM_BASES + 1, IN_FEAT, OUT_FEAT), dtype=jnp.float32, minval=-bound, maxval=bound)
        coeff = jax.random.normal(ks[5], (NUM_RELS, NUM_BASES), dtype=jnp.float32) * np.sqrt(2.0 / (NUM_RELS + NUM_BASES))
        h_bias = jnp.zeros((OUT_FEAT,), dtype=jnp.float32)
        loop_weight = jax.random.normal(ks[6], (IN_FEAT, OUT_FEAT), dtype=jnp.float32) * np.sqrt(2.0 / (IN_FEAT + OUT_FEAT))
        return {'feat': feat, 'coeff': coeff, 'W': W, 'h_bias': h_bias, 'loop_weight': loop_weight, 'edge_src': edge_src, 'edge_dst': edge_dst, 'etypes': etypes}
    _L1_gnn_all = _L1_gnn_setup()
    _L1_gnn_in = {k: v for k, v in _L1_gnn_all.items() if k in ('coeff', 'W', 'h_bias', 'loop_weight')}
    del _L1_gnn_all

    def _L2_gnn_setup():
        import jax, jax.numpy as jnp
        import numpy as np
        import math
        N = 6250
        E = 100000
        IN = 128
        H, C = (4, 32)
        ED = 16
        key = jax.random.key(seed)
        ks = jax.random.split(key, 12)
        s = 0.02
        return {'x': jax.random.normal(ks[0], (N, IN), jnp.float32), 'edge_attr': jax.random.normal(ks[1], (E, ED), jnp.float32), 'edge_index': jax.random.randint(ks[2], (2, E), 0, N, dtype=jnp.int32), 'Wq': jax.random.normal(ks[3], (IN, H * C), jnp.float32) * s, 'bq': jnp.zeros((H * C,), jnp.float32), 'Wk': jax.random.normal(ks[4], (IN, H * C), jnp.float32) * s, 'bk': jnp.zeros((H * C,), jnp.float32), 'Wv': jax.random.normal(ks[5], (IN, H * C), jnp.float32) * s, 'bv': jnp.zeros((H * C,), jnp.float32), 'We': jax.random.normal(ks[6], (ED, H * C), jnp.float32) * s, 'Wskip': jax.random.normal(ks[7], (IN, H * C), jnp.float32) * s, 'bskip': jnp.zeros((H * C,), jnp.float32), 'Wbeta': jax.random.normal(ks[8], (3 * H * C, 1), jnp.float32) * s}
    _L2_gnn_all = _L2_gnn_setup()
    _L2_gnn_in = {k: v for k, v in _L2_gnn_all.items() if k in ('Wq', 'bq', 'Wk', 'bk', 'Wv', 'bv', 'We', 'Wskip', 'bskip', 'Wbeta')}
    del _L2_gnn_all

    def _L3_gnn_setup():
        import jax, jax.numpy as jnp
        import numpy as np
        NC = 6250
        NT = 6250
        NNZ = 40000
        D = 128
        key = jax.random.key(seed)
        k1, k2, k3 = jax.random.split(key, 3)
        mat = jax.random.normal(k1, (NT, D), dtype=jnp.float32)
        row = jax.random.randint(k2, (NNZ,), 0, NC, dtype=jnp.int32)
        col = jax.random.randint(k3, (NNZ,), 0, NT, dtype=jnp.int32)
        return {'mat': mat, 'row': row, 'col': col}
    _L3_gnn_all = _L3_gnn_setup()
    _L3_gnn_in = {k: v for k, v in _L3_gnn_all.items() if k in ()}
    del _L3_gnn_all
    return {'x': x, 'src': src, 'dst': dst, 'edge_attr_16': edge_attr_16, 'edge_type_8': edge_type_8, 'L0_gnn_W_l': _L0_gnn_in['W_l'], 'L0_gnn_b_l': _L0_gnn_in['b_l'], 'L0_gnn_W_r': _L0_gnn_in['W_r'], 'L1_gnn_coeff': _L1_gnn_in['coeff'], 'L1_gnn_W': _L1_gnn_in['W'], 'L1_gnn_h_bias': _L1_gnn_in['h_bias'], 'L1_gnn_loop_weight': _L1_gnn_in['loop_weight'], 'L2_gnn_Wq': _L2_gnn_in['Wq'], 'L2_gnn_bq': _L2_gnn_in['bq'], 'L2_gnn_Wk': _L2_gnn_in['Wk'], 'L2_gnn_bk': _L2_gnn_in['bk'], 'L2_gnn_Wv': _L2_gnn_in['Wv'], 'L2_gnn_bv': _L2_gnn_in['bv'], 'L2_gnn_We': _L2_gnn_in['We'], 'L2_gnn_Wskip': _L2_gnn_in['Wskip'], 'L2_gnn_bskip': _L2_gnn_in['bskip'], 'L2_gnn_Wbeta': _L2_gnn_in['Wbeta']}

def reference(x, src, dst, edge_attr_16, edge_type_8, L0_gnn_W_l, L0_gnn_b_l, L0_gnn_W_r, L1_gnn_coeff, L1_gnn_W, L1_gnn_h_bias, L1_gnn_loop_weight, L2_gnn_Wq, L2_gnn_bq, L2_gnn_Wk, L2_gnn_bk, L2_gnn_Wv, L2_gnn_bv, L2_gnn_We, L2_gnn_Wskip, L2_gnn_bskip, L2_gnn_Wbeta):
    import jax
    import jax.numpy as jnp

    def _L0_gnn_ref(x, edge_index, W_l, b_l, W_r):
        import jax, jax.numpy as jnp
        import numpy as np
        N_NODES = 6250
        N_EDGES = 100000
        D_IN = 128
        D_OUT = 128
        src = edge_index[0]
        dst = edge_index[1]
        summed = jax.ops.segment_sum(x[src], dst, num_segments=N_NODES)
        count = jax.ops.segment_sum(jnp.ones((src.shape[0],), x.dtype), dst, num_segments=N_NODES)
        agg = summed / jnp.maximum(count, 1.0)[:, None]
        out = agg @ W_l.T + b_l + x @ W_r.T
        return out

    def _L1_gnn_ref(feat, coeff, W, h_bias, loop_weight, edge_src, edge_dst, etypes):
        import jax, jax.numpy as jnp
        import numpy as np
        N_NODES = 6250
        N_EDGES = 100000
        IN_FEAT = 128
        OUT_FEAT = 128
        NUM_RELS = 8
        NUM_BASES = 2
        n_dst = feat.shape[0]
        n_bases = coeff.shape[-1]
        msg = feat[edge_src]
        w = coeff[etypes]
        blocks = [feat[:n_dst]]
        for b in range(n_bases):
            blocks.append(jax.ops.segment_sum(w[:, b:b + 1] * msg, edge_dst, num_segments=n_dst))
        agg_out = jnp.concatenate(blocks, axis=-1)
        out = agg_out @ W.reshape(-1, W.shape[-1])
        h = out + h_bias + feat[:n_dst] @ loop_weight
        return h

    def _L2_gnn_ref(x, edge_attr, edge_index, Wq, bq, Wk, bk, Wv, bv, We, Wskip, bskip, Wbeta):
        import jax, jax.numpy as jnp
        import numpy as np
        import math
        N = 6250
        E = 100000
        IN = 128
        H, C = (4, 32)
        ED = 16
        n = x.shape[0]
        q = (x @ Wq + bq).reshape(n, H, C)
        k = (x @ Wk + bk).reshape(n, H, C)
        v = (x @ Wv + bv).reshape(n, H, C)
        row, col = (edge_index[0], edge_index[1])
        k_j = k[col] + (edge_attr @ We).reshape(-1, H, C)
        alpha = jnp.einsum('ehc,ehc->eh', q[row], k_j) / math.sqrt(C)
        m = jnp.zeros((n, H), alpha.dtype).at[row].set(alpha)
        ex = jnp.exp(alpha - m[row])
        denom = jax.ops.segment_sum(ex, row, num_segments=n)
        alpha = ex / (denom[row] + 1e-16)
        msgs = v[col] * alpha[..., None]
        out = jax.ops.segment_sum(msgs, row, num_segments=n)
        out = out.reshape(n, H * C)
        x_skip = x @ Wskip + bskip
        beta = jax.nn.sigmoid(jnp.concatenate([out, x_skip, out - x_skip], axis=-1) @ Wbeta)
        return beta * x_skip + (1.0 - beta) * out

    def _L3_gnn_ref(mat, row, col):
        import jax, jax.numpy as jnp
        import numpy as np
        NC = 6250
        NT = 6250
        NNZ = 40000
        D = 128
        vals = jnp.take(mat, col, axis=0)
        out = jax.ops.segment_sum(vals, row, num_segments=NC)
        return out
    edge_index = jnp.stack([src, dst])
    h = jnp.maximum(_layernorm(x, axis=-1), 0.0)
    x = x + _L0_gnn_ref(h, edge_index, L0_gnn_W_l, L0_gnn_b_l, L0_gnn_W_r)
    h = jnp.maximum(_layernorm(x, axis=-1), 0.0)
    x = x + _L1_gnn_ref(h, L1_gnn_coeff, L1_gnn_W, L1_gnn_h_bias, L1_gnn_loop_weight, src, dst, edge_type_8)
    h = jnp.maximum(_layernorm(x, axis=-1), 0.0)
    x = x + _L2_gnn_ref(h, edge_attr_16, edge_index, L2_gnn_Wq, L2_gnn_bq, L2_gnn_Wk, L2_gnn_bk, L2_gnn_Wv, L2_gnn_bv, L2_gnn_We, L2_gnn_Wskip, L2_gnn_bskip, L2_gnn_Wbeta)
    h = jnp.maximum(_layernorm(x, axis=-1), 0.0)
    x = x + _L3_gnn_ref(h, src, dst)
    return x

_drawn_inputs = setup_inputs


def setup_inputs(seed=0):
    import zlib

    import numpy as np

    out = dict(_drawn_inputs(seed))
    spreads = {'L0_gnn_b_l': (0.0, 0.1),
     'L1_gnn_h_bias': (0.0, 0.1),
     'L2_gnn_bq': (0.0, 0.1),
     'L2_gnn_bk': (0.0, 0.1),
     'L2_gnn_bv': (0.0, 0.1),
     'L2_gnn_bskip': (0.0, 0.1)}
    factors = {}
    for name, (base, spread) in spreads.items():
        noise = np.random.default_rng([zlib.crc32(name.encode()), seed]).standard_normal(out[name].shape)
        drawn = base * np.exp(spread * noise) if base else spread * noise
        out[name] = jnp.asarray(drawn.astype(out[name].dtype))
    for name, factor in factors.items():
        out[name] = (out[name] * factor).astype(out[name].dtype)
    return out
```

```python
import concourse.bass as bass
from concourse import mybir
from concourse.alu_op_type import AluOpType as ALU
from contextlib import ExitStack

F32 = mybir.dt.float32
I32 = mybir.dt.int32
U16 = mybir.dt.uint16
BF16 = mybir.dt.bfloat16
F16 = mybir.dt.float16
ACT = mybir.ActivationFunctionType
AX = mybir.AxisListType
ENGINE = mybir.EngineType

P = 128
N, D, E = 6250, 128, 200000
NB = -(-N // P)
NT = N - (NB - 1) * P
HEADS, HC, ED = 4, 32, 16
RELS, BASES = 8, 2
EP, EC = 125, 1600
NBIN = NB + 1
G = 8
TILES = -(-(E // P + NB) // (2 * G)) * 2 * G
GROUPS = TILES // G
ITERS = GROUPS // 2
WD = 4
WS = 3 + ED
QE = HEADS * ED
QW = D + QE + HEADS
SC = 16
CQ = EC // 4
LB = 7
GAP = 256
LN_EPS = 1e-5


class Chain:

    def __init__(self, eng, sem):
        self.eng, self.sem, self.n = eng, sem, 0

    def link(self, ins):
        ins.then_inc(self.sem, 1)
        self.n += 1
        self.eng.wait_ge(self.sem, self.n)


def wide(stat, rows=NB):
    return stat.unsqueeze(2).to_broadcast([P, rows, D])


def norm_vector(nc, dve, chain, stat, src, dst, tmp, var_ready, root_ready):
    chain.link(nc.vector.tensor_reduce(stat[:, 0, :], src[:], AX.X, ALU.add))
    chain.link(nc.vector.tensor_scalar(stat[:, 1, :], stat[:, 0, :], 1.0 / D, None, ALU.mult))
    chain.link(nc.vector.tensor_tensor(dst[:], src[:], wide(stat[:, 1, :]), ALU.subtract))
    chain.link(nc.vector.tensor_tensor(tmp[:], dst[:], dst[:], ALU.mult))
    chain.link(nc.vector.tensor_reduce(stat[:, 0, :], tmp[:], AX.X, ALU.add))
    nc.vector.tensor_scalar(stat[:, 2, :], stat[:, 0, :], 1.0 / D, None, ALU.mult).then_inc(var_ready, 1)
    dve.wait_ge(root_ready, 1)
    chain.link(nc.vector.reciprocal(stat[:, 1, :], stat[:, 3, :]))
    chain.link(nc.vector.tensor_tensor(tmp[:], dst[:], wide(stat[:, 1, :]), ALU.mult))
    chain.link(nc.vector.tensor_scalar(dst[:], tmp[:], 0.0, None, ALU.max))


def norm_scalar(nc, act, stat, eps, var_ready, root_ready):
    act.wait_ge(var_ready, 1)
    nc.scalar.activation(stat[:, 3, :], stat[:, 2, :], ACT.Sqrt, bias=eps[:, 0:1]).then_inc(root_ready, 1)


def stage_scalar(act, copies, staged, sent, first, last):
    def round_of(i):
        for s in range(2):
            copies(i, s, i * (2 * SC) + s * SC).then_inc(staged[s], 1)
    if first == 0:
        round_of(0)
    with act.Fori(max(first, 1), last) as i:
        for s in range(2):
            act.wait_ge(sent[s], i * (16 * SC))
            copies(i, s, i * (2 * SC) + s * SC).then_inc(staged[s], 1)


def scatter_pool(nc, pool, table, rows, words, staged, sent):
    with pool.Fori(0, EC // (2 * SC)) as i:
        for s in range(2):
            pool.wait_ge(staged[s], i + 1)
            pool.nop(nofuse=True)
            for j in range(SC):
                pool.indirect_dma_start(table, bass.IndirectOffsetOnAxis(ap=rows[:, s, j:j + 1], axis=0),
                                        words[:, s, j, :], None).then_inc(sent[s], 16)
    for s in range(2):
        pool.wait_ge(sent[s], 16 * EC // 2)


def blocks_of(nc, engine, table, first, count):
    _, values = nc.values_load_multi_w_load_instructions(
        table[0:1, bass.ds(first, count)], engines=(engine,), min_val=0, max_val=NB - 1,
        skip_runtime_bounds_check_because="the sort writes block numbers below NB")
    return values


def build(nc, x_in, src_in, dst_in, ea_in, et_in, wl_in, bl_in, wr_in, coeff_in, w1_in, hb_in, loop_in,
          wq_in, bq_in, wk_in, bk_in, wv_in, bv_in, we_in, wskip_in, bskip_in, wbeta_in, out):
    h_tab = nc.dram_tensor("h_tab", (NB * P, D), F32).ap()
    kv_tab = nc.dram_tensor("kv_tab", (NB * P, 2 * D), F32).ap()
    by_dst = nc.dram_tensor("by_dst", (TILES * P, WD), I32).ap()
    by_src = nc.dram_tensor("by_src", (TILES * P, WS), I32).ap()

    with ExitStack() as keep:
        def sb(name, shape, dt=F32, where=keep):
            return where.enter_context(nc.sbuf_tensor(name, list(shape), dt))

        x = sb("x", [P, NB, D])
        h = sb("h", [P, NB, D])
        tmp = sb("tmp", [P, NB, D])
        stat = sb("stat", [P, 4, NB])
        ident = sb("ident", [P, P])
        place = sb("place", [P, P])
        before = sb("before", [P, P], BF16)
        blk_dst = sb("blk_dst", [1, TILES], I32)
        blk_src = sb("blk_src", [1, TILES], I32)
        rep = sb("rep", [P, NB, WS - 1])
        eps = sb("eps", [P, 1])
        with ExitStack() as edges:
            edge = (sb("dst_i", [EP, EC], I32, edges),
                    sb("srcf", [EP, EC], F32, edges),
                    sb("dstf", [EP, EC], F32, edges),
                    sb("row_src", [EP, EC], I32, edges))
            sort_phase(nc, x_in, src_in, dst_in, et_in, coeff_in, x, h, tmp, stat, ident, place, before,
                       blk_dst, blk_src, eps, edge, h_tab, by_dst, by_src)
            with ExitStack() as sums0:
                acc = sb("acc0", [P, NB, D + 1], F32, sums0)
                sum_phase(nc, "l0", acc, D + 1, place, blk_dst, by_dst, WD, h_tab)
                mean_phase(nc, acc, x, h, tmp, stat, ident, eps, wl_in, bl_in, wr_in, h_tab, edge, ea_in, by_src)
        with ExitStack() as sums1:
            acc = sb("acc1", [P, NB, 2 * D], F32, sums1)
            acc3 = acc[:].rearrange("p b c -> p (b c)")[:, 0:NB * D].rearrange("p (b c) -> p b c", c=D)
            relation_phase(nc, acc, place, before, blk_dst, blk_src, by_dst, by_src, h_tab, rep)
            with ExitStack() as heads:
                qtab = sb("qtab", [P, NB, QW], F32, heads)
                skip = tmp
                project_phase(nc, acc, x, h, tmp, stat, ident, eps, w1_in, hb_in, loop_in, wq_in, bq_in, wk_in,
                              bk_in, wv_in, bv_in, we_in, wskip_in, bskip_in, kv_tab, qtab, skip)
                guard_phase(nc, acc, qtab, h, rep, kv_tab)
                att = acc[:].rearrange("p b c -> p (b c)")[:, 0:NB * (D + HEADS)].rearrange(
                    "p (b c) -> p b c", c=D + HEADS)
                attend_phase(nc, att, qtab, h, ident, place, blk_src, by_src, kv_tab)
                beta_phase(nc, att, skip, x, h, acc3, stat, eps, wbeta_in, h_tab)
            sum_phase(nc, "l3", acc3, D, place, blk_src, by_src, WS, h_tab)
            final_phase(nc, acc3, x, out)


def sort_phase(nc, x_in, src_in, dst_in, et_in, coeff_in, x, h, tmp, stat, ident, place, before,
               blk_dst, blk_src, eps, edge, h_tab, by_dst, by_src):
    dst_i, srcf, dstf, row_src = edge
    with ExitStack() as own:
        sb = lambda name, shape, dt=F32: own.enter_context(nc.sbuf_tensor(name, list(shape), dt))
        sem = lambda name: own.enter_context(nc.semaphore(name))
        src_i = sb("src_i", [EP, EC], I32)
        wordf = sb("wordf", [EP, EC, WD - 1])
        row_dst = sb("row_dst", [EP, EC], I32)
        coeff = sb("coeff", [P, RELS, BASES])
        is_rel = tmp[:].rearrange("p b d -> p (b d)")[0:EP, 0:EC]
        weighed = tmp[:].rearrange("p b d -> p (b d)")[0:EP, EC:2 * EC]
        binf = sb("binf", [EP, EC], BF16)
        onehot = [sb(f"onehot{s}", [EP, EC], BF16) for s in range(2)]
        cnt = sb("cnt", [P, EC])
        run = sb("run", [P, EC])
        int_a = sb("int_a", [P, EC], I32)
        int_b = sb("int_b", [P, EC], I32)
        start = sb("start", [P, EC], F16)
        sel = [sb(f"sel{s}", [P, EP], F16) for s in range(2)]
        ones = sb("ones", [P, P], F16)
        bins = sb("bins", [P, NBIN])
        hilo = sb("hilo", [P, NBIN])
        twice = sb("twice", [P, 320], BF16)
        lower = sb("lower", [P, P])
        tcol = sb("tcol", [P, 3])
        tint = sb("tint", [P, 2], I32)
        tile_no = sb("tile_no", [P, TILES])
        reached = sb("reached", [P, TILES], BF16)
        real = sb("real", [P, 1], BF16)
        zeros16 = sb("zeros16", [P, CQ], BF16)
        rows = sb("rows", [EP, 2, SC], I32)
        words = sb("words", [EP, 2, SC, WD], I32)
        banks = [own.enter_context(nc.psum_tensor(f"sort_ps{s}", [P, 4, 512], F32)) for s in range(2)]
        et_i = row_dst
        pos = run
        zero = h[:].rearrange("p b d -> p (b d)").bitcast(I32)

        x_loaded, idx_loaded, et_loaded, zeroed = sem("x_loaded"), sem("idx_loaded"), sem("et_loaded"), sem("zeroed")
        consts, built, zero_ready, x_padded = sem("consts"), sem("const_chain"), sem("zero_ready"), sem("x_padded")
        steps = sem("sort_steps")
        oh_ready = [sem(f"onehot_ready{s}") for s in range(2)]
        oh_used = [sem(f"onehot_used{s}") for s in range(2)]
        slot_used = [sem(f"slot_used{s}") for s in range(2)]
        cnt_ready, tiles_ready, base_ready = sem("cnt_ready"), sem("tiles_ready"), sem("base_ready")
        reached_ready, blk_ready, blk_used = sem("reached_ready"), sem("blk_ready"), sem("blk_used")
        sorted_dst = sem("sorted_dst")
        staged = [sem(f"staged_dst{s}") for s in range(2)]
        sent = [sem(f"sent_dst{s}") for s in range(2)]
        var_ready, root_ready, h_ready, h_stored = sem("var0"), sem("root0"), sem("h0_ready"), sem("h0_stored")

        ZD, ZS = TILES * WD, TILES * WS

        with nc.Block() as block:
            @block.sync
            def _(sp):
                sp.dma_start(dst_i[:], dst_in.rearrange("(p c) -> p c", p=EP)).then_inc(idx_loaded, 16)
                sp.dma_start(src_i[:], src_in.rearrange("(p c) -> p c", p=EP)).then_inc(idx_loaded, 16)
                sp.dma_start(et_i[:], et_in.rearrange("(p c) -> p c", p=EP)).then_inc(et_loaded, 16)
                sp.dma_start(coeff[:].rearrange("p r b -> p (r b)"),
                             coeff_in.rearrange("r b -> (r b)").unsqueeze(0).to_broadcast([P, RELS * BASES])
                             ).then_inc(et_loaded, 16)
                sp.wait_ge(x_padded, 1)
                sp.dma_start(x[:, 0:NB - 1, :], x_in[0:(NB - 1) * P, :].rearrange("(b p) d -> p b d", p=P)).then_inc(x_loaded, 16)
                sp.dma_start(x[0:NT, NB - 1, :], x_in[(NB - 1) * P:N, :]).then_inc(x_loaded, 16)
                sp.wait_ge(zero_ready, 1)
                dst_flat = by_dst.rearrange("(p r) w -> p (r w)", p=P)
                src_flat = by_src.rearrange("(p r) w -> p (r w)", p=P)
                for table, size in ((dst_flat, ZD), (src_flat, ZS)):
                    for at in range(0, size, NB * D):
                        n = min(NB * D, size - at)
                        sp.dma_start(table[:, at:at + n], zero[:, 0:n]).then_inc(zeroed, 16)
                sp.wait_ge(h_ready, 1)
                sp.dma_start(h_tab.rearrange("(b p) d -> p b d", p=P), h[:]).then_inc(h_stored, 16)
                sp.wait_ge(h_stored, 16)

            @block.gpsimd
            def _(pool):
                ch = Chain(pool, built)

                def keep_where(ap, op, fill, base, pattern, mult=1):
                    ch.link(nc.gpsimd.affine_select(out=ap, in_=ap, compare_op=op, fill=fill, base=base,
                                                    pattern=pattern, channel_multiplier=mult))
                ch.link(nc.gpsimd.memset(ident[:], 0.0))
                keep_where(ident[:], ALU.not_equal, 1.0, 0, [[-1, P]])
                for table, size, base in ((place, P, 1), (bins, NBIN, 0), (tile_no, TILES, 0)):
                    ch.link(nc.gpsimd.iota(table[:], pattern=[[1, size]], base=base, channel_multiplier=0,
                                           allow_small_or_imprecise_dtypes=True))
                ch.link(nc.gpsimd.memset(before[:], 1.0))
                keep_where(before[:], ALU.is_gt, 0.0, 0, [[1, P]], -1)
                ch.link(nc.gpsimd.memset(lower[:], 1.0))
                for half in range(2):
                    keep_where(lower[:, 64 * half:64 * half + 64], ALU.is_gt, 0.0, 0, [[1, 64]], -1)
                ch.link(nc.gpsimd.memset(hilo[:], 0.0))
                keep_where(hilo[:], ALU.not_equal, 256.0, 0, [[-1, NBIN]])
                keep_where(hilo[:], ALU.not_equal, 1.0, -64, [[-1, NBIN]])
                ch.link(nc.gpsimd.memset(twice[:], 0.0))
                ch.link(nc.gpsimd.memset(twice[:, 128:129], 1.0))
                ch.link(nc.gpsimd.memset(twice[:, 192:193], 1.0))
                ch.link(nc.gpsimd.memset(real[:], 1.0))
                keep_where(real[:], ALU.is_ge, 0.0, -1, [[0, 1]])
                keep_where(real[:], ALU.is_ge, 0.0, NB - 1, [[0, 1]], -1)
                ch.link(nc.gpsimd.memset(eps[:], LN_EPS))
                ch.link(nc.gpsimd.memset(zeros16[:], 0.0))
                nc.gpsimd.memset(ones[:], 1.0).then_inc(consts, 1)
                pool.wait_ge(zeroed, 16 * (-(-ZD // (NB * D)) + -(-ZS // (NB * D))))
                scatter_pool(nc, pool, by_dst, rows, words, staged, sent)

            @block.scalar
            def _(act):
                act.wait_ge(sorted_dst, 1)

                def copies(i, s, at):
                    nc.scalar.activation(rows[:, s, :], row_dst[:, bass.ds(at, SC)], ACT.Copy)
                    nc.scalar.activation(words[:, s, :, 0:1], src_i[:, bass.ds(at, SC)].unsqueeze(2), ACT.Copy)
                    return nc.scalar.activation(words[:].bitcast(F32)[:, s, :, 1:WD], wordf[:, bass.ds(at, SC), :], ACT.Copy)
                norm_scalar(nc, act, stat, eps, var_ready, root_ready)
                stage_scalar(act, copies, staged, sent, 0, EC // (2 * SC))

            @block.vector
            def _(dve):
                ch = Chain(dve, steps)
                for s in range(2):
                    dve.nop(nofuse=True).then_inc(oh_used[s], 1)
                    dve.nop(nofuse=True).then_inc(slot_used[s], 1)
                nc.vector.memset(x[:, NB - 1, :], 0.0).then_inc(x_padded, 1)
                nc.vector.memset(zero, 0).then_inc(zero_ready, 1)
                dve.wait_ge(idx_loaded, 32)
                dve.wait_ge(consts, 1)
                nc.vector.tensor_copy(dstf[:], dst_i[:])

                def sort(turn, key, place_out, row_out, blk):
                    ch.link(nc.vector.tensor_scalar(int_a[0:EP, :], key[:], 7, None, ALU.logical_shift_right))
                    ch.link(nc.vector.tensor_scalar(int_b[0:EP, :], key[:], P - 1, None, ALU.bitwise_and))
                    ch.link(nc.vector.tensor_copy(binf[:], int_a[0:EP, :]))
                    ch.link(nc.vector.tensor_scalar(place_out, int_b[0:EP, :].unsqueeze(2), 1.0, None, ALU.add))
                    half = NBIN // 2
                    with dve.Fori(0, half) as i:
                        for s in range(2):
                            dve.wait_ge(oh_used[s], i + (turn * 2 * half + 1))
                            nc.vector.tensor_scalar(onehot[s][:], binf[:], bins[0:EP, bass.ds(2 * i + s, 1)], None,
                                                    ALU.is_equal).then_inc(oh_ready[s], 1)
                    dve.wait_ge(cnt_ready, turn + 1)
                    ch.link(nc.vector.tensor_copy(cnt[:].rearrange("p (c q) -> p c q", c=4), banks[0][:, :, 0:CQ]))
                    ch.link(nc.vector.memset(int_b[:], 0))
                    ch.link(nc.vector.tensor_tensor_scan(run[:], cnt[:], int_b[:].bitcast(F32), 0.0, ALU.add, ALU.add))
                    ch.link(nc.vector.tensor_tensor(cnt[:], run[:], cnt[:], ALU.subtract))
                    ch.link(nc.vector.tensor_scalar(tint[:, 0:1], run[:, EC - 1:EC], float(P - 1), None, ALU.add))
                    ch.link(nc.vector.tensor_scalar(tint[:, 1:2], tint[:, 0:1], 7, None, ALU.logical_shift_right))
                    nc.vector.tensor_copy(tcol[:, 0:1], tint[:, 1:2]).then_inc(tiles_ready, 1)
                    dve.wait_ge(base_ready, turn + 1)
                    ch.link(nc.vector.tensor_copy(tcol[:, 1:2], banks[1][:, 0, 0:1]))
                    nc.vector.tensor_scalar(reached[:], tile_no[:], tcol[:, 1:2], None, ALU.is_ge).then_inc(reached_ready, 1)
                    ch.link(nc.vector.tensor_scalar(tcol[:, 2:3], tcol[:, 1:2], float(P), None, ALU.mult))
                    ch.link(nc.vector.tensor_scalar(int_a[:], cnt[:], tcol[:, 2:3], None, ALU.add))
                    ch.link(nc.vector.tensor_scalar(int_b[0:64, :], int_a[0:64, :], 8, None, ALU.logical_shift_right))
                    ch.link(nc.vector.tensor_scalar(int_b[64:P, :], int_a[64:P, :], 255, None, ALU.bitwise_and))
                    ch.link(nc.vector.tensor_copy(start[:], int_b[:]))
                    dve.wait_ge(blk_ready, turn + 1)
                    nc.vector.tensor_copy(blk[:].rearrange("p (c q) -> p c q", c=4), banks[1][0:1, :, 0:TILES // 4]).then_inc(blk_used, 1)
                    with dve.Fori(0, half) as i:
                        for s in range(2):
                            dve.wait_ge(slot_used[s], i + (turn * half + 1))
                            nc.vector.tensor_scalar(sel[s][:], ones[:, 0:EP], hilo[:, bass.ds(2 * i + s, 1)], None, ALU.mult)
                            nc.vector.tensor_scalar(onehot[s][:], binf[:], bins[0:EP, bass.ds(2 * i + s, 1)], None,
                                                    ALU.is_equal).then_inc(oh_ready[s], 1)
                        for s in range(2):
                            dve.wait_ge(oh_used[s], i + (turn * 2 * half + half + 2))
                            if s:
                                dve.wait_ge(slot_used[0], i + (turn * half + 2))
                            else:
                                dve.wait_ge(slot_used[1], i + (turn * half + 1))
                            dve.nop(nofuse=True)
                            nc.vector.copy_predicated(pos[0:EP, :].rearrange("p (c q) -> p c q", c=4),
                                                      onehot[s][:].bitcast(U16).rearrange("p (c q) -> p c q", c=4),
                                                      banks[s][0:EP, :, 0:CQ]).then_inc(slot_used[s], 1)
                    dve.wait_ge(slot_used[1], (turn + 1) * half + 1)
                    a, b = int_a[0:EP, :], int_b[0:EP, :]
                    c = int_p[0:EP, :]
                    ch.link(nc.vector.tensor_copy(c, pos[0:EP, :]))
                    ch.link(nc.vector.tensor_scalar(a, c, 10, 10, ALU.logical_shift_right, ALU.logical_shift_left))
                    ch.link(nc.vector.tensor_scalar(b, c, P - 1, 3, ALU.bitwise_and, ALU.logical_shift_left))
                    ch.link(nc.vector.tensor_tensor(a, a, b, ALU.bitwise_or))
                    ch.link(nc.vector.tensor_scalar(b, c, 7, G - 1, ALU.logical_shift_right, ALU.bitwise_and))
                    ch.link(nc.vector.tensor_tensor(row_out[:], a, b, ALU.bitwise_or))

                int_p = cnt[:].bitcast(I32)
                dve.wait_ge(et_loaded, 32)
                for b in range(BASES):
                    for r in range(RELS):
                        ch.link(nc.vector.tensor_scalar(is_rel, et_i[:], float(r), None, ALU.is_equal))
                        w = wordf[:, :, 1 + b]
                        if r == 0:
                            ch.link(nc.vector.tensor_scalar(w, is_rel, coeff[0:EP, r, b:b + 1], None, ALU.mult))
                        else:
                            ch.link(nc.vector.scalar_tensor_tensor(w, is_rel, coeff[0:EP, r, b:b + 1], w, ALU.mult, ALU.add))
                sort(0, dst_i, wordf[:, :, 0:1], row_dst, blk_dst)
                nc.vector.memset(tcol[:, 0:1], 0.0).then_inc(sorted_dst, 1)
                dve.wait_ge(x_loaded, 32)
                dve.wait_ge(zeroed, 16 * (-(-ZD // (NB * D)) + -(-ZS // (NB * D))))
                norm_vector(nc, dve, ch, stat, x, h, tmp, var_ready, root_ready)
                nc.vector.memset(tcol[:, 0:1], 0.0).then_inc(h_ready, 1)
                sort(1, src_i, srcf[:].unsqueeze(2), row_src, blk_src)

            @block.tensor
            def _(pe):
                pe.wait_ge(consts, 1)
                half = NBIN // 2
                for turn in range(2):
                    if turn:
                        pe.wait_ge(slot_used[1], turn * half + 1)
                        pe.wait_ge(slot_used[0], turn * half + 1)
                    for c in range(4):
                        nc.tensor.matmul(banks[0][:, c, 0:CQ], twice[:, 0:P], zeros16[:], start=True, stop=False)
                    with pe.Fori(0, half) as i:
                        for s in range(2):
                            pe.wait_ge(oh_ready[s], i + turn * 2 * half + 1)
                            pe.nop(nofuse=True)
                            for c in range(4):
                                last = nc.tensor.matmul(banks[0][:, c, 0:CQ], twice[0:EP, bass.ds((P - s) - i * 2, P)],
                                                        onehot[s][:, c * CQ:(c + 1) * CQ], start=False, stop=False)
                            last.then_inc(oh_used[s], 1)
                    for c in range(4):
                        last = nc.tensor.matmul(banks[0][:, c, 0:CQ], twice[:, 0:P], zeros16[:], start=False, stop=True)
                    last.then_inc(cnt_ready, 1)
                    pe.wait_ge(tiles_ready, turn + 1)
                    nc.tensor.matmul(banks[1][:, 0, 0:1], lower[:], tcol[:, 0:1], start=True, stop=True).then_inc(base_ready, 1)
                    pe.wait_ge(reached_ready, turn + 1)
                    for c in range(4):
                        last = nc.tensor.matmul(banks[1][0:1, c, 0:TILES // 4], real[:], reached[:, c * (TILES // 4):(c + 1) * (TILES // 4)],
                                                start=True, stop=True)
                    last.then_inc(blk_ready, 1)
                    pe.wait_ge(blk_used, turn + 1)
                    pe.nop(nofuse=True)
                    with pe.Fori(0, half) as i:
                        for s in range(2):
                            pe.wait_ge(oh_ready[s], i + turn * 2 * half + half + 1)
                            pe.wait_ge(slot_used[s], i + (turn * half + 1))
                            for c in range(4):
                                cut = slice(c * CQ, (c + 1) * CQ)
                                nc.tensor.matmul(banks[s][0:EP, c, 0:CQ], before[0:EP, 0:EP], onehot[s][:, cut], start=True, stop=False)
                                last = nc.tensor.matmul(banks[s][0:EP, c, 0:CQ], sel[s][:], start[:, cut], start=False, stop=True)
                            last.then_inc(oh_used[s], 1)


def load_group(sp, table, words, g, ready):
    rows = table.rearrange("(g r) w -> g (r w)", r=P * G)
    sp.dma_start(words[:].rearrange("p j w -> p (j w)"),
                 rows[bass.ds(g, 1), :].rearrange("a (p c) -> (a p) c", p=P)).then_inc(ready, 16)


def gather_group(pool, table, words, rows, width, ready):
    for j in range(G):
        pool.indirect_dma_start(rows[:, j, 0:width], None, table,
                                bass.IndirectOffsetOnAxis(ap=words[:, j, 0:1], axis=0)).then_inc(ready, 16)


def one_hot(nc, dve_out, place, places, tiles):
    return nc.vector.tensor_tensor(dve_out, place[:].unsqueeze(1).to_broadcast([P, tiles, P]),
                                   places.to_broadcast([P, tiles, P]), ALU.is_equal)


def sum_phase(nc, tag, acc, cols, place, blk, sorted_edges, width, table):
    T2 = 2 * G
    with ExitStack() as own:
        sb = lambda name, shape, dt=F32: own.enter_context(nc.sbuf_tensor(f"{tag}_{name}", list(shape), dt))
        sem = lambda name: own.enter_context(nc.semaphore(f"{tag}_{name}"))
        words = [sb(f"words{s}", [P, G, width], I32) for s in range(2)]
        rows = [sb(f"rows{s}", [P, G, cols]) for s in range(2)]
        onehot = [sb(f"onehot{s}", [P, G, P]) for s in range(2)]
        sums = [own.enter_context(nc.psum_tensor(f"{tag}_sums{s}", [P, G, GAP], F32)) for s in range(2)]
        words_ready = [sem(f"words_ready{s}") for s in range(2)]
        rows_ready = [sem(f"rows_ready{s}") for s in range(2)]
        oh_ready, summed, added = sem("onehot_ready"), sem("summed"), sem("added")
        at = 1 if width == WD else 2

        with nc.Block() as block:
            @block.sync
            def _(sp):
                with sp.Fori(0, ITERS) as i:
                    for s in range(2):
                        sp.wait_ge(summed, i * T2 + (s * G + G))
                        load_group(sp, sorted_edges, words[s], 2 * i + s, words_ready[s])

            @block.gpsimd
            def _(pool):
                with pool.Fori(0, ITERS) as i:
                    for s in range(2):
                        pool.wait_ge(words_ready[s], i * 16 + 16)
                        pool.wait_ge(summed, i * T2 + (s * G + G))
                        pool.nop(nofuse=True)
                        gather_group(pool, table, words[s], rows[s], D, rows_ready[s])

            @block.vector
            def _(dve):
                if cols > D:
                    for s in range(2):
                        nc.vector.memset(rows[s][:, :, D:cols], 1.0)
                nc.vector.memset(acc[:], 0.0).then_inc(added, T2)
                dve.nop(nofuse=True).then_inc(summed, T2)
                with dve.Fori(0, ITERS) as i:
                    for s in range(2):
                        dve.wait_ge(words_ready[s], i * 16 + 16)
                        one_hot(nc, onehot[s][:], place, words[s][:].bitcast(F32)[:, :, at:at + 1], G).then_inc(oh_ready, 1)
                        blocks = blocks_of(nc, ENGINE.DVE, blk, i * T2 + s * G, G)
                        for j in range(G):
                            if j % 2 == 0:
                                dve.wait_ge(summed, i * T2 + (s * G + j + 2 + T2))
                            dve.wait_ge(added, i * T2 + (s * G + j + T2))
                            a = acc[:, bass.ds(blocks[j], 1), :]
                            nc.vector.tensor_tensor(a, a, sums[s][:, j:j + 1, 0:cols], ALU.add).then_inc(added, 1)

            @block.tensor
            def _(pe):
                with pe.Fori(0, ITERS) as i:
                    for s in range(2):
                        pe.wait_ge(oh_ready, i * 2 + (s + 1))
                        pe.wait_ge(rows_ready[s], i * (16 * G) + 16 * G)
                        for j in range(G):
                            if j % 2 == 0:
                                pe.wait_ge(added, i * T2 + (s * G + j + 2))
                            nc.tensor.matmul(sums[s][:, j, 0:cols], onehot[s][:, j, :], rows[s][:, j, :],
                                             start=True, stop=True).then_inc(summed, 1)


def mean_phase(nc, acc, x, h, tmp, stat, ident, eps, wl_in, bl_in, wr_in, h_tab, edge, ea_in, by_src):
    dst_i, srcf, dstf, row_src = edge
    with ExitStack() as own:
        sb = lambda name, shape, dt=F32: own.enter_context(nc.sbuf_tensor(f"l0n_{name}", list(shape), dt))
        sem = lambda name: own.enter_context(nc.semaphore(f"l0n_{name}"))
        ps = lambda name: own.enter_context(nc.psum_tensor(f"l0n_{name}", [P, LB + 1, P], F32))
        w_raw = sb("w_raw", [P, 2, D])
        wT = sb("wT", [P, 2, D])
        bias = sb("bias", [P, D])
        a7, h7 = sb("a7", [P, LB, D]), sb("h7", [P, LB, D])
        aT, hT = sb("aT", [P, LB, P]), sb("hT", [P, LB, P])
        ps_a, ps_h, ps_o = ps("ps_a"), ps("ps_h"), ps("ps_o")
        rows = sb("rows", [EP, 2, SC], I32)
        attr = [sb(f"attr{s}", [EP, SC, ED]) for s in range(2)]
        words = sb("words", [EP, 2, SC, WS], I32)
        staged = [sem(f"staged{s}") for s in range(2)]
        sent = [sem(f"sent{s}") for s in range(2)]
        attr_ready = [sem(f"attr_ready{s}") for s in range(2)]
        w_loaded, wT_ready, wT_copied, steps = sem("w_loaded"), sem("wT_ready"), sem("wT_copied"), sem("steps")
        taken, turned, copied, product, summed = sem("taken"), sem("turned"), sem("copied"), sem("product"), sem("summed")
        var_ready, root_ready, h_ready, h_stored = sem("var"), sem("root"), sem("h_ready"), sem("h_stored")
        rounds = EC // (2 * SC)

        with nc.Block() as block:
            @block.sync
            def _(sp):
                sp.dma_start(w_raw[:, 0, :], wl_in).then_inc(w_loaded, 16)
                sp.dma_start(w_raw[:, 1, :], wr_in).then_inc(w_loaded, 16)
                sp.dma_start(bias[:], bl_in.unsqueeze(0).to_broadcast([P, D])).then_inc(w_loaded, 16)
                ea = ea_in.rearrange("(p c) w -> p (c w)", p=EP)
                for s in range(2):
                    sp.dma_start(attr[s][:].rearrange("p c w -> p (c w)"),
                                 ea[:, s * SC * ED:(s + 1) * SC * ED]).then_inc(attr_ready[s], 16)

                def attributes(i):
                    for s in range(2):
                        sp.wait_ge(staged[s], i)
                        sp.dma_start(attr[s][:].rearrange("p c w -> p (c w)"),
                                     ea[:, bass.ds(i * (2 * SC * ED) + s * SC * ED, SC * ED)]).then_inc(attr_ready[s], 16)
                with sp.Fori(1, rounds // 2) as i:
                    attributes(i)
                sp.wait_ge(h_ready, 1)
                sp.dma_start(h_tab.rearrange("(b p) d -> p b d", p=P), h[:]).then_inc(h_stored, 16)
                with sp.Fori(rounds // 2, rounds) as i:
                    attributes(i)
                sp.wait_ge(h_stored, 16)

            @block.gpsimd
            def _(pool):
                scatter_pool(nc, pool, by_src, rows, words, staged, sent)

            @block.scalar
            def _(act):
                wf = words[:].bitcast(F32)

                def copies(i, s, at):
                    act.wait_ge(attr_ready[s], i * 16 + 16)
                    nc.scalar.activation(rows[:, s, :], row_src[:, bass.ds(at, SC)], ACT.Copy)
                    nc.scalar.activation(words[:, s, :, 0:1], dst_i[:, bass.ds(at, SC)].unsqueeze(2), ACT.Copy)
                    nc.scalar.activation(wf[:, s, :, 1:2], dstf[:, bass.ds(at, SC)].unsqueeze(2), ACT.Copy)
                    nc.scalar.activation(wf[:, s, :, 2:3], srcf[:, bass.ds(at, SC)].unsqueeze(2), ACT.Copy)
                    return nc.scalar.activation(wf[:, s, :, 3:WS], attr[s][:], ACT.Copy)
                stage_scalar(act, copies, staged, sent, 0, rounds // 2)
                norm_scalar(nc, act, stat, eps, var_ready, root_ready)
                stage_scalar(act, copies, staged, sent, rounds // 2, rounds)

            @block.vector
            def _(dve):
                ch = Chain(dve, steps)
                ch.link(nc.vector.tensor_scalar(stat[:, 0, :].unsqueeze(2), acc[:, :, D:D + 1], 1.0, None, ALU.max))
                ch.link(nc.vector.reciprocal(stat[:, 1, :], stat[:, 0, :]))
                dve.nop(nofuse=True).then_inc(turned, 1)
                dve.wait_ge(wT_ready, 1)
                nc.vector.tensor_copy(wT[:], ps_o[:, 0:2, :]).then_inc(wT_copied, 1)
                dve.wait_ge(w_loaded, 48)
                ch.link(nc.vector.tensor_tensor(x[:], x[:], bias[:].unsqueeze(1).to_broadcast([P, NB, D]), ALU.add))
                with dve.Fori(0, NB // LB) as i:
                    here = bass.ds(i * LB, LB)
                    dve.wait_ge(turned, i + 1)
                    nc.vector.tensor_tensor(a7[:], acc[:, here, 0:D], stat[:, 1, here].unsqueeze(2).to_broadcast([P, LB, D]), ALU.mult)
                    nc.vector.tensor_copy(h7[:], h[:, here, :]).then_inc(taken, 1)
                    dve.wait_ge(turned, i + 2)
                    nc.vector.tensor_copy(aT[:], ps_a[:, 0:LB, :])
                    nc.vector.tensor_copy(hT[:], ps_h[:, 0:LB, :]).then_inc(copied, 1)
                    dve.wait_ge(product, i + 1)
                    nc.vector.tensor_tensor(x[:, here, :], x[:, here, :], ps_o[:, 0:LB, :], ALU.add).then_inc(summed, 1)
                dve.wait_ge(summed, NB // LB)
                norm_vector(nc, dve, ch, stat, x, h, tmp, var_ready, root_ready)
                nc.vector.memset(stat[:, 0, 0:1], 0.0).then_inc(h_ready, 1)

            @block.tensor
            def _(pe):
                pe.wait_ge(w_loaded, 48)
                for k in range(2):
                    last = nc.tensor.transpose(ps_o[:, k, :], w_raw[:, k, :], ident[:])
                last.then_inc(wT_ready, 1)
                pe.wait_ge(wT_copied, 1)
                pe.nop(nofuse=True)
                with pe.Fori(0, NB // LB) as i:
                    pe.wait_ge(taken, i + 1)
                    for src, dst in ((a7, ps_a), (h7, ps_h)):
                        for j in range(LB):
                            last = nc.tensor.transpose(dst[:, j, :], src[:, j, :], ident[:])
                    last.then_inc(turned, 1)
                    pe.wait_ge(copied, i + 1)
                    for j in range(LB):
                        nc.tensor.matmul(ps_o[:, j, :], aT[:, j, :], wT[:, 0, :], start=True, stop=False)
                        last = nc.tensor.matmul(ps_o[:, j, :], hT[:, j, :], wT[:, 1, :], start=False, stop=True)
                    last.then_inc(product, 1)


def relation_phase(nc, acc, place, before, blk_dst, blk_src, by_dst, by_src, h_tab, rep):
    T2 = 2 * G
    with ExitStack() as own:
        sb = lambda name, shape, dt=F32: own.enter_context(nc.sbuf_tensor(f"l1_{name}", list(shape), dt))
        sem = lambda name: own.enter_context(nc.semaphore(f"l1_{name}"))
        ps = lambda name, shape: own.enter_context(nc.psum_tensor(f"l1_{name}", shape, F32))
        words_d = [sb(f"words_d{s}", [P, G, WD], I32) for s in range(2)]
        words_s = [sb(f"words_s{s}", [P, G, WS], I32) for s in range(2)]
        rows = [sb(f"rows{s}", [P, G, D]) for s in range(2)]
        msg = sb("msg", [P, G, 2 * D])
        onehot = sb("onehot", [P, G, P])
        onehot_s = sb("onehot_s", [P, G, P], BF16)
        first = sb("first", [P, G, P])
        unseen = sb("unseen", [P, NB, 1])
        sums = ps("sums", [P, G, GAP])
        rank = ps("rank", [P, G, P])
        pick = ps("pick", [P, G, 32])
        dready = [sem(f"words_d_ready{s}") for s in range(2)]
        sready = [sem(f"words_s_ready{s}") for s in range(2)]
        rows_ready = [sem(f"rows_ready{s}") for s in range(2)]
        cleared, scaled, summed, added = sem("cleared"), sem("scaled"), sem("summed"), sem("added")
        oh_ready, ohs_ready, ranked, firsts, picked, kept = (
            sem("onehot_ready"), sem("onehot_s_ready"), sem("ranked"), sem("firsts"), sem("picked"), sem("kept"))

        with nc.Block() as block:
            @block.sync
            def _(sp):
                with sp.Fori(0, ITERS) as i:
                    for s in range(2):
                        sp.wait_ge(added, i * T2 + (s * G + G))
                        load_group(sp, by_dst, words_d[s], 2 * i + s, dready[s])
                        sp.wait_ge(kept, i * (2 * T2) + (2 * s * G + 2 * G))
                        load_group(sp, by_src, words_s[s], 2 * i + s, sready[s])

            @block.gpsimd
            def _(pool):
                with pool.Fori(0, ITERS) as i:
                    for s in range(2):
                        pool.wait_ge(dready[s], i * 16 + 16)
                        pool.wait_ge(scaled, i * T2 + (s * G + G))
                        pool.nop(nofuse=True)
                        gather_group(pool, h_tab, words_d[s], rows[s], D, rows_ready[s])

            @block.scalar
            def _(act):
                with act.Fori(0, ITERS) as i:
                    for s in range(2):
                        act.wait_ge(rows_ready[s], i * (16 * G) + 16 * G)
                        act.wait_ge(summed, i * T2 + (s * G + G))
                        for j in range(G):
                            for b in range(BASES):
                                last = nc.scalar.activation(msg[:, j, b * D:(b + 1) * D], rows[s][:, j, :], ACT.Copy,
                                                            scale=words_d[s][:].bitcast(F32)[:, j, 2 + b:3 + b])
                            last.then_inc(scaled, 1)

            @block.vector
            def _(dve):
                nc.vector.memset(rep[:], 0.0).then_inc(cleared, 1)
                nc.vector.memset(unseen[:], 1.0).then_inc(kept, 2 * T2)
                nc.vector.memset(acc[:], 0.0).then_inc(added, T2)
                dve.nop(nofuse=True).then_inc(scaled, T2)
                dve.nop(nofuse=True).then_inc(summed, G)
                dve.wait_ge(cleared, 1)
                with dve.Fori(0, ITERS) as i:
                    for s in range(2):
                        blocks_d = blocks_of(nc, ENGINE.DVE, blk_dst, i * T2 + s * G, G)
                        blocks_s = blocks_of(nc, ENGINE.DVE, blk_src, i * T2 + s * G, G)
                        dve.wait_ge(sready[s], i * 16 + 16)
                        one_hot(nc, onehot_s[:], place, words_s[s][:].bitcast(F32)[:, :, 2:3], G).then_inc(ohs_ready, 1)
                        dve.wait_ge(dready[s], i * 16 + 16)
                        one_hot(nc, onehot[:], place, words_d[s][:].bitcast(F32)[:, :, 1:2], G).then_inc(oh_ready, 1)
                        for q in range(2):
                            cut = slice(q * G // 2, (q + 1) * G // 2)
                            dve.wait_ge(ranked, i * 4 + 2 * s + q + 1)
                            nc.vector.scalar_tensor_tensor(first[:, cut, :], rank[:, cut, :], 0.0, onehot_s[:, cut, :],
                                                           ALU.is_equal, ALU.mult).then_inc(firsts, 1)
                        for j in range(G):
                            t = i * T2 + (s * G + j)
                            r = rep[:, bass.ds(blocks_s[j], 1), :]
                            u = unseen[:, bass.ds(blocks_s[j], 1), :].rearrange("p a o -> p (a o)")
                            if j == 0:
                                dve.wait_ge(picked, i * 2 + s + 1)
                            dve.wait_ge(kept, t * 2 + 2 * T2)
                            nc.vector.scalar_tensor_tensor(r, pick[:, j:j + 1, 0:WS - 1], u, r, ALU.mult, ALU.add).then_inc(kept, 1)
                            if j % 2 == 0:
                                dve.wait_ge(summed, t + (2 + G))
                            dve.wait_ge(added, t + T2)
                            a = acc[:, bass.ds(blocks_d[j], 1), :]
                            nc.vector.tensor_tensor(a, a, sums[:, j:j + 1, :], ALU.add).then_inc(added, 1)
                            dve.wait_ge(kept, t * 2 + (2 * T2 + 1))
                            nc.vector.scalar_tensor_tensor(u, pick[:, j, 1:2], 0.0, u, ALU.is_equal, ALU.mult).then_inc(kept, 1)

            @block.tensor
            def _(pe):
                with pe.Fori(0, ITERS) as i:
                    for s in range(2):
                        pe.wait_ge(ohs_ready, i * 2 + s + 1)
                        for j in range(G):
                            last = nc.tensor.matmul(rank[:, j, :], before[:], onehot_s[:, j, :], start=True, stop=True)
                            if j % (G // 2) == G // 2 - 1:
                                last.then_inc(ranked, 1)
                        for j in range(G):
                            if j % (G // 2) == 0:
                                pe.wait_ge(firsts, i * 4 + 2 * s + j // (G // 2) + 1)
                            last = nc.tensor.matmul(pick[:, j, 0:WS - 1], first[:, j, :], words_s[s][:].bitcast(F32)[:, j, 1:WS],
                                                    start=True, stop=True)
                        last.then_inc(picked, 1)
                        pe.wait_ge(oh_ready, i * 2 + s + 1)
                        for j in range(G):
                            if j % 2 == 0:
                                pe.wait_ge(added, i * T2 + (s * G + j + 2 + G))
                            pe.wait_ge(scaled, i * T2 + (s * G + j + 1 + T2))
                            nc.tensor.matmul(sums[:, j, :], onehot[:, j, :], msg[:, j, :], start=True, stop=True).then_inc(summed, 1)


def project_phase(nc, acc, x, h, tmp, stat, ident, eps, w1_in, hb_in, loop_in, wq_in, bq_in, wk_in, bk_in,
                  wv_in, bv_in, we_in, wskip_in, bskip_in, kv_tab, qtab, skip):
    QS = D + QE + D
    with ExitStack() as own:
        sb = lambda name, shape, dt=F32: own.enter_context(nc.sbuf_tensor(f"l2p_{name}", list(shape), dt))
        sem = lambda name: own.enter_context(nc.semaphore(f"l2p_{name}"))
        w1 = sb("w1", [P, 4, D])
        bias1 = sb("bias1", [P, D])
        wqs = sb("wqs", [P, QS])
        wkv = sb("wkv", [P, 2 * D])
        bqs = sb("bqs", [P, QS])
        bkv = sb("bkv", [P, 2 * D])
        we = sb("we", [ED, D])
        bq_col = sb("bq_col", [P, 1])
        bq_wide = sb("bq_wide", [P, P])
        wqT, weT = sb("wqT", [P, P]), sb("weT", [P, ED])
        we_heads = sb("we_heads", [P, QE])
        room = qtab[:].rearrange("p b c -> p (b c)")
        in7, inT = (room[:, k * 3 * LB * D:(k + 1) * 3 * LB * D].rearrange("p (k b d) -> p k b d", k=3, b=LB) for k in range(2))
        h7, hT = sb("h7", [P, LB, D]), sb("hT", [P, LB, P])
        loaded, summed_w, wT, wT_copied, wqe, ready = (sem(n) for n in ("loaded", "w_summed", "wT", "wT_copied", "wqe", "weights_ready"))
        steps, taken, turned, copied, product, summed = (sem(n) for n in ("steps", "taken", "turned", "copied", "product", "summed"))
        var_ready, root_ready, h_ready = sem("var"), sem("root"), sem("h_ready")
        taken2, turned2, copied2, qs_ready, kv_ready, qs_read, kv_read, kv_stored = (
            sem(n) for n in ("taken2", "turned2", "copied2", "qs_ready", "kv_ready", "qs_read", "kv_read", "kv_stored"))
        LOADS = 14
        R = NB // LB

        def first_half():
            with ExitStack() as mem:
                ps_i = [mem.enter_context(nc.psum_tensor(f"l2p_ps_i{k}", [P, LB + 1, P], F32)) for k in range(3)]
                ps_o = mem.enter_context(nc.psum_tensor("l2p_ps_o", [P, LB + 1, P], F32))
                with nc.Block() as block:
                    @block.sync
                    def _(sp):
                        def load(to, of):
                            sp.dma_start(to, of).then_inc(loaded, 16)
                        for k in range(3):
                            load(w1[:, k, :], w1_in[k])
                        load(w1[:, 3, :], loop_in)
                        load(bias1[:], hb_in.unsqueeze(0).to_broadcast([P, D]))
                        load(wqs[:, 0:D], wq_in)
                        load(wqs[:, D + QE:QS], wskip_in)
                        load(wkv[:, 0:D], wk_in)
                        load(wkv[:, D:2 * D], wv_in)
                        load(we[:], we_in)
                        load(bqs[:, 0:D], bq_in.unsqueeze(0).to_broadcast([P, D]))
                        load(bqs[:, D + QE:QS], bskip_in.unsqueeze(0).to_broadcast([P, D]))
                        load(bkv[:, 0:D], bk_in.unsqueeze(0).to_broadcast([P, D]))
                        load(bkv[:, D:2 * D], bv_in.unsqueeze(0).to_broadcast([P, D]))
                        load(bq_col[:], bq_in.unsqueeze(1))

                    @block.scalar
                    def _(act):
                        with act.Fori(0, R) as i:
                            here = bass.ds(i * LB, LB)
                            act.wait_ge(turned, i + 1)
                            nc.scalar.activation(in7[:, 0], h[:, here, :], ACT.Copy)
                            nc.scalar.activation(in7[:, 1], acc[:, here, 0:D], ACT.Copy)
                            nc.scalar.activation(in7[:, 2], acc[:, here, D:2 * D], ACT.Copy).then_inc(taken, 1)
                        norm_scalar(nc, act, stat, eps, var_ready, root_ready)

                    @block.vector
                    def _(dve):
                        ch = Chain(dve, steps)
                        dve.nop(nofuse=True).then_inc(turned, 1)
                        dve.wait_ge(loaded, 16 * (LOADS + 1))
                        ch.link(nc.vector.tensor_tensor(w1[:, 0, :], w1[:, 0, :], w1[:, 3, :], ALU.add))
                        ch.link(nc.vector.memset(we_heads[:], 0.0))
                        nc.vector.tensor_copy(bq_wide[:], bq_col[:].to_broadcast([P, P]))
                        dve.wait_ge(wT, 1)
                        nc.vector.tensor_copy(wqT[:], ps_o[:, 0, :])
                        for k in range(HEADS):
                            part = slice(k * HC, (k + 1) * HC)
                            last = nc.vector.tensor_copy(we_heads[part, k * ED:(k + 1) * ED], ps_o[part, 4, 0:ED])
                        last.then_inc(wT_copied, 1)
                        dve.wait_ge(wqe, 1)
                        nc.vector.tensor_copy(wqs[:, D:D + QE], ps_o[:, 0, 0:QE])
                        nc.vector.tensor_copy(bqs[:, D:D + QE], ps_o[:, 4, 0:QE]).then_inc(ready, 1)
                        ch.link(nc.vector.tensor_tensor(x[:], x[:], bias1[:].unsqueeze(1).to_broadcast([P, NB, D]), ALU.add))
                        with dve.Fori(0, R) as i:
                            here = bass.ds(i * LB, LB)
                            dve.wait_ge(turned, i + 2)
                            for k in range(3):
                                last = nc.vector.tensor_copy(inT[:, k], ps_i[k][:, 0:LB, :])
                            last.then_inc(copied, 1)
                            dve.wait_ge(product, i + 1)
                            nc.vector.tensor_tensor(x[:, here, :], x[:, here, :], ps_o[:, 0:LB, :], ALU.add).then_inc(summed, 1)
                        dve.wait_ge(summed, R)
                        norm_vector(nc, dve, ch, stat, x, h, tmp, var_ready, root_ready)

                    @block.tensor
                    def _(pe):
                        pe.wait_ge(loaded, 16 * (LOADS + 1))
                        nc.tensor.transpose(ps_o[:, 0, :], wqs[:, 0:D], ident[:])
                        nc.tensor.transpose(ps_o[:, 4, 0:ED], we[:], ident[0:ED, 0:ED]).then_inc(wT, 1)
                        pe.wait_ge(wT_copied, 1)
                        nc.tensor.matmul(ps_o[:, 0, 0:QE], wqT[:], we_heads[:], start=True, stop=True)
                        nc.tensor.matmul(ps_o[:, 4, 0:QE], bq_wide[:], we_heads[:], start=True, stop=True).then_inc(wqe, 1)
                        pe.wait_ge(ready, 1)
                        pe.nop(nofuse=True)
                        with pe.Fori(0, R) as i:
                            pe.wait_ge(taken, i + 1)
                            for k in range(3):
                                for j in range(LB):
                                    last = nc.tensor.transpose(ps_i[k][:, j, :], in7[:, k, j, :], ident[:])
                            last.then_inc(turned, 1)
                            pe.wait_ge(copied, i + 1)
                            for j in range(LB):
                                for k in range(3):
                                    last = nc.tensor.matmul(ps_o[:, j, :], inT[:, k, j, :], w1[:, k, :], start=(k == 0), stop=(k == 2))
                            last.then_inc(product, 1)

        def second_half():
            with ExitStack() as mem:
                ps_t = mem.enter_context(nc.psum_tensor("l2p_ps_t", [P, LB + 1, P], F32))
                ps_qs = [mem.enter_context(nc.psum_tensor(f"l2p_qs{k}", [P, 512], F32)) for k in range(3)]
                ps_kv = [mem.enter_context(nc.psum_tensor(f"l2p_kv{k}", [P, 512], F32)) for k in range(3)]
                with nc.Block() as block:
                    @block.sync
                    def _(sp):
                        rows = kv_tab.rearrange("(r b p) c -> r p b c", b=LB, p=P)
                        with sp.Fori(0, R) as i:
                            sp.wait_ge(kv_read, i * LB + (LB + 1))
                            sp.dma_start(rows[bass.ds(i, 1)].rearrange("a p b c -> (a p) b c"), acc[:, bass.ds(i * LB, LB), :]).then_inc(kv_stored, 16)
                        sp.wait_ge(kv_stored, 16 * R)

                    @block.scalar
                    def _(act):
                        for n in (turned2, kv_ready, kv_read):
                            act.nop(nofuse=True).then_inc(n, 1)
                        with act.Fori(0, R) as i:
                            act.wait_ge(turned2, i + 1)
                            nc.scalar.activation(h7[:], h[:, bass.ds(i * LB, LB), :], ACT.Copy).then_inc(taken2, 1)
                            act.wait_ge(turned2, i + 2)
                            act.wait_ge(kv_ready, i * LB + 1)
                            nc.scalar.activation(hT[:], ps_t[:, 0:LB, :], ACT.Copy).then_inc(copied2, 1)

                    @block.vector
                    def _(dve):
                        with dve.Fori(0, R) as i:
                            for j in range(LB):
                                b = bass.ds(i * LB + j, 1)
                                dve.wait_ge(qs_ready, i * LB + j + 1)
                                qs = ps_qs[j % 3][:].unsqueeze(1)
                                nc.vector.tensor_tensor(qtab[:, b, 0:D + QE], qs[:, :, 0:D + QE], bqs[:, 0:D + QE].unsqueeze(1), ALU.add)
                                nc.vector.tensor_tensor(skip[:, b, :], qs[:, :, D + QE:QS], bqs[:, D + QE:QS].unsqueeze(1), ALU.add).then_inc(qs_read, 1)
                                dve.wait_ge(kv_ready, i * LB + (j + 2))
                                nc.vector.tensor_tensor(acc[:, b, :], ps_kv[j % 3][:, 0:2 * D].unsqueeze(1), bkv[:].unsqueeze(1), ALU.add).then_inc(kv_read, 1)

                    @block.tensor
                    def _(pe):
                        with pe.Fori(0, R) as i:
                            pe.wait_ge(taken2, i + 1)
                            for j in range(LB):
                                last = nc.tensor.transpose(ps_t[:, j, :], h7[:, j, :], ident[:])
                            last.then_inc(turned2, 1)
                            pe.wait_ge(copied2, i + 1)
                            for j in range(LB):
                                if j < 3:
                                    pe.wait_ge(kv_read, i * LB + 1)
                                else:
                                    pe.wait_ge(kv_read, i * LB + (j - 1))
                                nc.tensor.matmul(ps_qs[j % 3][:, 0:QS], hT[:, j, :], wqs[:], start=True, stop=True).then_inc(qs_ready, 1)
                                nc.tensor.matmul(ps_kv[j % 3][:, 0:2 * D], hT[:, j, :], wkv[:], start=True, stop=True).then_inc(kv_ready, 1)

        first_half()
        second_half()


def guard_phase(nc, acc, qtab, tmp, rep, kv_tab):
    with ExitStack() as own:
        sb = lambda name, shape, dt=F32: own.enter_context(nc.sbuf_tensor(f"l2g_{name}", list(shape), dt))
        sem = lambda name: own.enter_context(nc.semaphore(f"l2g_{name}"))
        idx = sb("idx", [P, NB, 1], I32)
        part = sb("part", [P, 2, NB, HEADS])
        idx_ready, rows_ready, steps = sem("idx_ready"), sem("rows_ready"), sem("steps")
        with nc.Block() as block:
            @block.gpsimd
            def _(pool):
                pool.wait_ge(idx_ready, 1)
                pool.nop(nofuse=True)
                for b in range(NB):
                    pool.indirect_dma_start(acc[:, b, :], None, kv_tab, bass.IndirectOffsetOnAxis(ap=idx[:, b, :], axis=0)
                                            ).then_inc(rows_ready, 16)

            @block.vector
            def _(dve):
                ch = Chain(dve, steps)
                nc.vector.tensor_copy(idx[:], rep[:, :, 0:1]).then_inc(idx_ready, 1)
                by_head = tmp[:, :, 0:QE].rearrange("p b (n e) -> p b n e", n=HEADS)
                for k in range(HEADS):
                    last = nc.vector.tensor_tensor(by_head[:, :, k, :], qtab[:, :, D + k * ED:D + (k + 1) * ED], rep[:, :, 2:WS - 1], ALU.mult)
                ch.link(last)
                ch.link(nc.vector.tensor_reduce(part[:, 0], by_head, AX.X, ALU.add))
                dve.wait_ge(rows_ready, 16 * NB)
                ch.link(nc.vector.tensor_tensor(tmp[:], qtab[:, :, 0:D], acc[:, :, 0:D], ALU.mult))
                ch.link(nc.vector.tensor_reduce(part[:, 1], tmp[:].rearrange("p b (n c) -> p b n c", n=HEADS), AX.X, ALU.add))
                ch.link(nc.vector.tensor_tensor(qtab[:, :, D + QE:QW], part[:, 0], part[:, 1], ALU.add))


def attend_phase(nc, acc, qtab, h, ident, place, blk, by_src, kv_tab):
    T2, Q = 2 * G, G // 2
    SCALE = HC ** -0.5
    C = D + HEADS
    with ExitStack() as own:
        sb = lambda name, shape, dt=F32: own.enter_context(nc.sbuf_tensor(f"l2_{name}", list(shape), dt))
        sem = lambda name: own.enter_context(nc.semaphore(f"l2_{name}"))
        ps = lambda name, shape: own.enter_context(nc.psum_tensor(f"l2_{name}", shape, F32))
        words = [sb(f"words{s}", [P, G, WS], I32) for s in range(2)]
        kv = [sb(f"kv{s}", [P, G, 2 * D]) for s in range(2)]
        room, used = h[:].rearrange("p b d -> p (b d)"), [0]

        def carve(tiles, size):
            at = used[0]
            used[0] += tiles * size
            return room[:, at:at + tiles * size].rearrange("p (t c) -> p t c", t=tiles)
        onehot = [carve(G, P) for s in range(2)]
        turned = [carve(Q, P) for q in range(2)]
        msg = [carve(Q, C) for q in range(2)]
        prod = carve(Q, HEADS * (HC + ED)).rearrange("p t (n c) -> p t n c", n=HEADS)
        score = [sb(f"score{q}", [P, 2, Q, HEADS]) for q in range(2)]
        ps_t = [ps(f"ps_t{q}", [P, Q, P]) for q in range(2)]
        ps_q = [ps(f"ps_q{q}", [P, Q, GAP]) for q in range(2)]
        ps_s = ps("ps_s", [P, Q, GAP])
        words_ready = [sem(f"words_ready{s}") for s in range(2)]
        kv_ready = [sem(f"kv_ready{s}") for s in range(2)]
        names = ("onehot_ready", "flipped", "flip_copied", "queried", "multiplied", "scored", "exped", "msg_ready", "summed", "added", "steps")
        oh_ready, flipped, flip_copied, queried, multiplied, scored, exped, msg_ready, summed, added, steps = (sem(n) for n in names)

        HALVES = 2 * GROUPS

        def half(m):
            return m // 2 % 2, m % 2

        def steps_of(eng, step):
            step(0, 0)
            rounds = (HALVES - 1) // 4
            with eng.Fori(0, rounds) as i:
                for n in range(1, 5):
                    step(i, n)
            for m in range(4 * rounds + 1, HALVES):
                step(rounds, m - 4 * rounds)

        def last_of(i, n, ahead):
            return isinstance(i, int) and 4 * i + n + ahead >= HALVES

        with nc.Block() as block:
            @block.sync
            def _(sp):
                for s in range(2):
                    load_group(sp, by_src, words[s], s, words_ready[s])
                with sp.Fori(1, ITERS) as i:
                    for s in range(2):
                        sp.wait_ge(scored, i * 4 + (2 * s - 2))
                        load_group(sp, by_src, words[s], 2 * i + s, words_ready[s])

            @block.gpsimd
            def _(pool):
                for s in range(2):
                    pool.wait_ge(words_ready[s], 16)
                    pool.nop(nofuse=True)
                    gather_group(pool, kv_tab, words[s], kv[s], 2 * D, kv_ready[s])
                with pool.Fori(1, ITERS) as i:
                    for s in range(2):
                        pool.wait_ge(words_ready[s], i * 16 + 16)
                        pool.wait_ge(msg_ready, i * 4 + (2 * s - 2))
                        pool.nop(nofuse=True)
                        gather_group(pool, kv_tab, words[s], kv[s], 2 * D, kv_ready[s])

            @block.scalar
            def _(act):
                def flip_copy(i, n):
                    act.wait_ge(flipped, 4 * i + (n + 1))
                    nc.scalar.activation(turned[n % 2], ps_t[n % 2][:], ACT.Copy).then_inc(flip_copied, 1)

                def step(i, n):
                    if not last_of(i, n, 1):
                        flip_copy(i, n + 1)
                    q = n % 2
                    act.wait_ge(scored, 4 * i + (n + 1))
                    nc.scalar.activation(msg[q][:, :, D:C], score[q][:, 1], ACT.Exp, scale=SCALE).then_inc(exped, 1)
                flip_copy(0, 0)
                steps_of(act, step)

            @block.vector
            def _(dve):
                nc.vector.memset(acc, 0.0).then_inc(added, G)

                def one_hots(i, n):
                    s, q = half(n)
                    cut = slice(q * Q, (q + 1) * Q)
                    if q == 0:
                        dve.wait_ge(words_ready[s], (i + n // 4) * 16 + 16)
                    one_hot(nc, onehot[s][:, cut, :], place, words[s][:].bitcast(F32)[:, cut, 2:3], Q).then_inc(oh_ready, 1)

                def add(i, n, e, blocks):
                    if e % 2 == 0:
                        dve.wait_ge(summed, i * T2 + (n * Q + e + 2))
                    dve.wait_ge(added, i * T2 + (n * Q + e + G))
                    a = acc[:, bass.ds(blocks[e], 1), :]
                    nc.vector.tensor_tensor(a, a, ps_s[:, e:e + 1, 0:C], ALU.add).then_inc(added, 1)

                def step(i, n):
                    s, q = half(n)
                    cut = slice(q * Q, (q + 1) * Q)
                    first = isinstance(i, int) and 4 * i + n == 0
                    heads = lambda ap, c: ap.rearrange("p t (n c) -> p t n c", n=HEADS)
                    blocks = None if first else blocks_of(nc, ENGINE.DVE, blk, i * T2 + (n - 1) * Q, Q)

                    def add_before(e):
                        if not first:
                            add(i, n - 1, e, blocks)
                    sc = score[q]
                    dve.wait_ge(queried, 4 * i + (n + 1))
                    if q == 0:
                        dve.wait_ge(kv_ready[s], (i + n // 4) * (16 * G) + 16 * G)
                    nc.vector.tensor_tensor(prod[:, :, :, 0:HC], heads(ps_q[q][:, :, 0:D], HC), heads(kv[s][:, cut, 0:D], HC), ALU.mult)
                    add_before(0)
                    nc.vector.tensor_tensor(prod[:, :, :, HC:HC + ED], heads(ps_q[q][:, :, D:D + QE], ED),
                                            words[s][:].bitcast(F32)[:, cut, 3:WS].unsqueeze(2).to_broadcast([P, Q, HEADS, ED]),
                                            ALU.mult).then_inc(multiplied, 1)
                    add_before(1)
                    dve.wait_ge(multiplied, 4 * i + (n + 1))
                    nc.vector.tensor_reduce(sc[:, 0], prod, AX.X, ALU.add).then_inc(steps, 1)
                    add_before(2)
                    dve.wait_ge(steps, 4 * i + (n + 1))
                    nc.vector.tensor_tensor(sc[:, 1], sc[:, 0], ps_q[q][:, :, D + QE:QW], ALU.subtract).then_inc(scored, 1)
                    add_before(3)
                    if not last_of(i, n, 2):
                        one_hots(i, n + 2)
                    dve.wait_ge(exped, 4 * i + (n + 1))
                    nc.vector.tensor_tensor(heads(msg[q][:, :, 0:D], HC), heads(kv[s][:, cut, D:2 * D], HC),
                                            msg[q][:, :, D:C].unsqueeze(3).to_broadcast([P, Q, HEADS, HC]),
                                            ALU.mult).then_inc(msg_ready, 1)
                one_hots(0, 0)
                one_hots(0, 1)
                steps_of(dve, step)
                blocks = blocks_of(nc, ENGINE.DVE, blk, TILES - Q, Q)
                for e in range(Q):
                    add(0, HALVES - 1, e, blocks)

            @block.tensor
            def _(pe):
                def flip(i, n):
                    s, q = half(n)
                    pe.wait_ge(oh_ready, 4 * i + (n + 1))
                    for e in range(Q):
                        last = nc.tensor.transpose(ps_t[q][:, e, :], onehot[s][:, q * Q + e, :], ident[:])
                    last.then_inc(flipped, 1)

                def sum_up(i, n):
                    s, q = half(n)
                    pe.wait_ge(msg_ready, 4 * i + (n + 1))
                    for e in range(Q):
                        nc.tensor.matmul(ps_s[:, e, 0:C], onehot[s][:, q * Q + e, :], msg[q][:, e, :], start=True, stop=True).then_inc(summed, 1)

                def step(i, n):
                    q = n % 2
                    blocks = blocks_of(nc, ENGINE.PE, blk, i * T2 + n * Q, Q)
                    pe.wait_ge(flip_copied, 4 * i + (n + 1))
                    for e in range(Q):
                        last = nc.tensor.matmul(ps_q[q][:, e, 0:QW], turned[q][:, e, :],
                                                qtab[:, bass.ds(blocks[e], 1), :].rearrange("p a c -> p (a c)"), start=True, stop=True)
                    last.then_inc(queried, 1)
                    if not last_of(i, n, 1):
                        flip(i, n + 1)
                    if not (isinstance(i, int) and 4 * i + n == 0):
                        sum_up(i, n - 1)
                flip(0, 0)
                steps_of(pe, step)
                sum_up(0, HALVES - 1)


def beta_phase(nc, acc, skip, x, h, tmp, stat, eps, wbeta_in, h_tab):
    with ExitStack() as own:
        sb = lambda name, shape, dt=F32: own.enter_context(nc.sbuf_tensor(f"l2b_{name}", list(shape), dt))
        sem = lambda name: own.enter_context(nc.semaphore(f"l2b_{name}"))
        wb = sb("wb", [P, 3, D])
        wz = sb("wz", [P, 2, D])
        rden = sb("rden", [P, NB, HEADS])
        z = sb("z", [P, 4, NB])
        loaded, steps, z_ready, e_ready = sem("loaded"), sem("steps"), sem("z_ready"), sem("exp_ready")
        var_ready, root_ready, h_ready, h_stored = sem("var"), sem("root"), sem("h_ready"), sem("h_stored")
        att = h
        with nc.Block() as block:
            @block.sync
            def _(sp):
                sp.dma_start(wb[:].rearrange("p k d -> p (k d)"),
                             wbeta_in.rearrange("k o -> (k o)").unsqueeze(0).to_broadcast([P, 3 * D])).then_inc(loaded, 16)
                sp.wait_ge(h_ready, 1)
                sp.dma_start(h_tab.rearrange("(b p) d -> p b d", p=P), h[:]).then_inc(h_stored, 16)
                sp.wait_ge(h_stored, 16)

            @block.scalar
            def _(act):
                act.wait_ge(z_ready, 1)
                nc.scalar.activation(z[:, 1, :], z[:, 0, :], ACT.Exp, scale=-1.0).then_inc(e_ready, 1)
                norm_scalar(nc, act, stat, eps, var_ready, root_ready)

            @block.vector
            def _(dve):
                ch = Chain(dve, steps)
                ch.link(nc.vector.tensor_scalar(rden[:], acc[:, :, D:D + HEADS], 1e-16, None, ALU.add))
                ch.link(nc.vector.reciprocal(rden[:], rden[:]))
                for k in range(HEADS):
                    part = slice(k * HC, (k + 1) * HC)
                    last = nc.vector.tensor_tensor(att[:, :, part], acc[:, :, part], rden[:, :, k:k + 1].to_broadcast([P, NB, HC]), ALU.mult)
                ch.link(last)
                dve.wait_ge(loaded, 16)
                nc.vector.tensor_tensor(wz[:, 0, :], wb[:, 0, :], wb[:, 2, :], ALU.add)
                ch.link(nc.vector.tensor_tensor(wz[:, 1, :], wb[:, 1, :], wb[:, 2, :], ALU.subtract))
                for k, part in enumerate((att, skip)):
                    ch.link(nc.vector.tensor_tensor(tmp[:], part[:], wz[:, k, :].unsqueeze(1).to_broadcast([P, NB, D]), ALU.mult))
                    ch.link(nc.vector.tensor_reduce(z[:, 2 + k, :], tmp[:], AX.X, ALU.add))
                nc.vector.tensor_tensor(z[:, 0, :], z[:, 2, :], z[:, 3, :], ALU.add).then_inc(z_ready, 1)
                ch.link(nc.vector.tensor_tensor(skip[:], skip[:], att[:], ALU.subtract))
                ch.link(nc.vector.tensor_tensor(x[:], x[:], att[:], ALU.add))
                dve.wait_ge(e_ready, 1)
                ch.link(nc.vector.tensor_scalar(z[:, 2, :], z[:, 1, :], 1.0, None, ALU.add))
                ch.link(nc.vector.reciprocal(z[:, 3, :], z[:, 2, :]))
                ch.link(nc.vector.tensor_tensor(skip[:], skip[:], wide(z[:, 3, :]), ALU.mult))
                ch.link(nc.vector.tensor_tensor(x[:], x[:], skip[:], ALU.add))
                norm_vector(nc, dve, ch, stat, x, h, tmp, var_ready, root_ready)
                nc.vector.memset(z[:, 0, 0:1], 0.0).then_inc(h_ready, 1)


def final_phase(nc, acc, x, out):
    with nc.semaphore("last_sum") as done, nc.semaphore("out_stored") as stored:
        with nc.Block() as block:
            @block.vector
            def _(dve):
                nc.vector.tensor_tensor(x[:], x[:], acc, ALU.add).then_inc(done, 1)

            @block.sync
            def _(sp):
                sp.wait_ge(done, 1)
                sp.dma_start(out[0:(NB - 1) * P, :].rearrange("(b p) d -> p b d", p=P), x[:, 0:NB - 1, :]).then_inc(stored, 16)
                sp.dma_start(out[(NB - 1) * P:N, :], x[0:NT, NB - 1, :]).then_inc(stored, 16)
                sp.wait_ge(stored, 32)


_INS = ["x", "src", "dst", "edge_attr_16", "edge_type_8", "L0_gnn_W_l", "L0_gnn_b_l", "L0_gnn_W_r", "L1_gnn_coeff",
        "L1_gnn_W", "L1_gnn_h_bias", "L1_gnn_loop_weight", "L2_gnn_Wq", "L2_gnn_bq", "L2_gnn_Wk", "L2_gnn_bk",
        "L2_gnn_Wv", "L2_gnn_bv", "L2_gnn_We", "L2_gnn_Wskip", "L2_gnn_bskip", "L2_gnn_Wbeta"]


def kernel(**inputs):
    import numpy as _np
    import concourse.bacc as _bacc
    from concourse import mybir as _mybir
    from concourse.bass_utils import run_bass_kernel_spmd as _run

    nc = _bacc.Bacc("TRN2", target_bir_lowering=False, num_devices=1)
    arrays, args = {}, []
    for name in _INS:
        a = _np.ascontiguousarray(inputs[name])
        arrays[f"in_{name}"] = a
        args.append(nc.dram_tensor(f"in_{name}", a.shape, _mybir.dt.from_np(a.dtype), kind="ExternalInput").ap())
    args.append(nc.dram_tensor("out_x", (N, D), _mybir.dt.float32, kind="ExternalOutput").ap())
    build(nc, *args)
    r = _run(nc, [arrays], core_ids=[0])
    return r.results[0]["out_x"]
```

```python
import concourse.bass as bass
from concourse import mybir
from concourse.alu_op_type import AluOpType as ALU
from contextlib import ExitStack

F32 = mybir.dt.float32
I32 = mybir.dt.int32
U16 = mybir.dt.uint16
BF16 = mybir.dt.bfloat16
F16 = mybir.dt.float16
ACT = mybir.ActivationFunctionType
AX = mybir.AxisListType
ENGINE = mybir.EngineType

P = 128
N, D, E = 6250, 128, 200000
NB = -(-N // P)
NT = N - (NB - 1) * P
HEADS, HC, ED = 4, 32, 16
RELS, BASES = 8, 2
EP, EC = 125, 1600
NBIN = NB + 1
G = 8
TILES = -(-(E // P + NB) // (2 * G)) * 2 * G
GROUPS = TILES // G
ITERS = GROUPS // 2
WD = 4
WS = 3 + ED
QE = HEADS * ED
QW = D + QE + HEADS
SC = 16
CQ = EC // 4
LB = 7
GAP = 256
LN_EPS = 1e-5


class Chain:

    def __init__(self, eng, sem):
        self.eng, self.sem, self.n = eng, sem, 0

    def link(self, ins):
        ins.then_inc(self.sem, 1)
        self.n += 1
        self.eng.wait_ge(self.sem, self.n)


def wide(stat, rows=NB):
    return stat.unsqueeze(2).to_broadcast([P, rows, D])


def norm_vector(nc, dve, chain, stat, src, dst, tmp, var_ready, root_ready):
    chain.link(nc.vector.tensor_reduce(stat[:, 0, :], src[:], AX.X, ALU.add))
    chain.link(nc.vector.tensor_scalar(stat[:, 1, :], stat[:, 0, :], 1.0 / D, None, ALU.mult))
    chain.link(nc.vector.tensor_tensor(dst[:], src[:], wide(stat[:, 1, :]), ALU.subtract))
    chain.link(nc.vector.tensor_tensor(tmp[:], dst[:], dst[:], ALU.mult))
    chain.link(nc.vector.tensor_reduce(stat[:, 0, :], tmp[:], AX.X, ALU.add))
    nc.vector.tensor_scalar(stat[:, 2, :], stat[:, 0, :], 1.0 / D, None, ALU.mult).then_inc(var_ready, 1)
    dve.wait_ge(root_ready, 1)
    chain.link(nc.vector.reciprocal(stat[:, 1, :], stat[:, 3, :]))
    chain.link(nc.vector.tensor_tensor(tmp[:], dst[:], wide(stat[:, 1, :]), ALU.mult))
    chain.link(nc.vector.tensor_scalar(dst[:], tmp[:], 0.0, None, ALU.max))


def norm_scalar(nc, act, stat, eps, var_ready, root_ready):
    act.wait_ge(var_ready, 1)
    nc.scalar.activation(stat[:, 3, :], stat[:, 2, :], ACT.Sqrt, bias=eps[:, 0:1]).then_inc(root_ready, 1)


def stage_scalar(act, copies, staged, sent, first, last):
    def round_of(i):
        for s in range(2):
            copies(i, s, i * (2 * SC) + s * SC).then_inc(staged[s], 1)
    if first == 0:
        round_of(0)
    with act.Fori(max(first, 1), last) as i:
        for s in range(2):
            act.wait_ge(sent[s], i * (16 * SC))
            copies(i, s, i * (2 * SC) + s * SC).then_inc(staged[s], 1)


def scatter_pool(nc, pool, table, rows, words, staged, sent):
    with pool.Fori(0, EC // (2 * SC)) as i:
        for s in range(2):
            pool.wait_ge(staged[s], i + 1)
            pool.nop(nofuse=True)
            for j in range(SC):
                pool.indirect_dma_start(table, bass.IndirectOffsetOnAxis(ap=rows[:, s, j:j + 1], axis=0),
                                        words[:, s, j, :], None).then_inc(sent[s], 16)
    for s in range(2):
        pool.wait_ge(sent[s], 16 * EC // 2)


def blocks_of(nc, engine, table, first, count):
    _, values = nc.values_load_multi_w_load_instructions(
        table[0:1, bass.ds(first, count)], engines=(engine,), min_val=0, max_val=NB - 1,
        skip_runtime_bounds_check_because="the sort writes block numbers below NB")
    return values


def build(nc, x_in, src_in, dst_in, ea_in, et_in, wl_in, bl_in, wr_in, coeff_in, w1_in, hb_in, loop_in,
          wq_in, bq_in, wk_in, bk_in, wv_in, bv_in, we_in, wskip_in, bskip_in, wbeta_in, out):
    h_tab = nc.dram_tensor("h_tab", (NB * P, D), F32).ap()
    kv_tab = nc.dram_tensor("kv_tab", (NB * P, 2 * D), F32).ap()
    by_dst = nc.dram_tensor("by_dst", (TILES * P, WD), I32).ap()
    by_src = nc.dram_tensor("by_src", (TILES * P, WS), I32).ap()

    with ExitStack() as keep:
        def sb(name, shape, dt=F32, where=keep):
            return where.enter_context(nc.sbuf_tensor(name, list(shape), dt))

        x = sb("x", [P, NB, D])
        h = sb("h", [P, NB, D])
        tmp = sb("tmp", [P, NB, D])
        stat = sb("stat", [P, 4, NB])
        ident = sb("ident", [P, P])
        place = sb("place", [P, P])
        minus = sb("minus", [P, P])
        before = sb("before", [P, P], BF16)
        blk_dst = sb("blk_dst", [1, TILES], I32)
        blk_src = sb("blk_src", [1, TILES], I32)
        rep = sb("rep", [P, NB, WS - 1])
        eps = sb("eps", [P, 1])
        with ExitStack() as edges:
            edge = (sb("dst_i", [EP, EC], I32, edges),
                    sb("srcf", [EP, EC], F32, edges),
                    sb("dstf", [EP, EC], F32, edges),
                    sb("row_src", [EP, EC], I32, edges))
            sort_phase(nc, x_in, src_in, dst_in, et_in, coeff_in, x, h, tmp, stat, ident, place, minus, before,
                       blk_dst, blk_src, eps, edge, h_tab, by_dst, by_src)
            with ExitStack() as sums0:
                acc = sb("acc0", [P, NB, D + 1], F32, sums0)
                sum_phase(nc, "l0", acc, D + 1, place, blk_dst, by_dst, WD, h_tab)
                mean_phase(nc, acc, x, h, tmp, stat, ident, eps, wl_in, bl_in, wr_in, h_tab, edge, ea_in, by_src)
        with ExitStack() as sums1:
            acc = sb("acc1", [P, NB, 2 * D], F32, sums1)
            acc3 = acc[:].rearrange("p b c -> p (b c)")[:, 0:NB * D].rearrange("p (b c) -> p b c", c=D)
            relation_phase(nc, acc, place, minus, before, blk_dst, blk_src, by_dst, by_src, h_tab, rep)
            with ExitStack() as heads:
                qtab = sb("qtab", [P, NB, QW], F32, heads)
                skip = tmp
                project_phase(nc, acc, x, h, tmp, stat, ident, eps, w1_in, hb_in, loop_in, wq_in, bq_in, wk_in,
                              bk_in, wv_in, bv_in, we_in, wskip_in, bskip_in, kv_tab, qtab, skip)
                att = acc[:].rearrange("p b c -> p (b c)")[:, 0:NB * (D + HEADS)].rearrange(
                    "p (b c) -> p b c", c=D + HEADS)
                attend_phase(nc, acc, att, qtab, h, rep, ident, place, blk_src, by_src, kv_tab)
                beta_phase(nc, att, skip, x, h, acc3, stat, eps, wbeta_in, h_tab)
            sum_phase(nc, "l3", acc3, D, minus, blk_src, by_src, WS, h_tab)
            final_phase(nc, acc3, x, out)


def sort_phase(nc, x_in, src_in, dst_in, et_in, coeff_in, x, h, tmp, stat, ident, place, minus, before,
               blk_dst, blk_src, eps, edge, h_tab, by_dst, by_src):
    dst_i, srcf, dstf, row_src = edge
    with ExitStack() as own:
        sb = lambda name, shape, dt=F32: own.enter_context(nc.sbuf_tensor(name, list(shape), dt))
        sem = lambda name: own.enter_context(nc.semaphore(name))
        src_i = sb("src_i", [EP, EC], I32)
        wordf = sb("wordf", [EP, EC, WD - 1])
        row_dst = sb("row_dst", [EP, EC], I32)
        coeff = sb("coeff", [P, RELS, BASES])
        is_rel = tmp[:].rearrange("p b d -> p (b d)")[0:EP, 0:EC]
        binf = sb("binf", [EP, EC], BF16)
        onehot = [sb(f"onehot{s}", [EP, EC], BF16) for s in range(2)]
        cnt = sb("cnt", [P, EC])
        run = sb("run", [P, EC])
        int_a = sb("int_a", [P, EC], I32)
        int_b = sb("int_b", [P, EC], I32)
        start = sb("start", [P, EC], F16)
        sel = [sb(f"sel{s}", [P, EP], F16) for s in range(2)]
        ones = sb("ones", [P, P], F16)
        bins = sb("bins", [P, NBIN])
        hilo = sb("hilo", [P, NBIN])
        twice = sb("twice", [P, 320], BF16)
        lower = sb("lower", [P, P])
        tcol = sb("tcol", [P, 3])
        tint = sb("tint", [P, 2], I32)
        tile_no = sb("tile_no", [P, TILES])
        reached = sb("reached", [P, TILES], BF16)
        real = sb("real", [P, 1], BF16)
        zeros16 = sb("zeros16", [P, CQ], BF16)
        rows = sb("rows", [EP, 2, SC], I32)
        words = sb("words", [EP, 2, SC, WD], I32)
        banks = [own.enter_context(nc.psum_tensor(f"sort_ps{s}", [P, 4, 512], F32)) for s in range(2)]
        et_i = row_dst
        pos = run
        zero = h[:].rearrange("p b d -> p (b d)").bitcast(I32)

        x_loaded, idx_loaded, et_loaded, zeroed = sem("x_loaded"), sem("idx_loaded"), sem("et_loaded"), sem("zeroed")
        consts, built, zero_ready, x_padded = sem("consts"), sem("const_chain"), sem("zero_ready"), sem("x_padded")
        steps = sem("sort_steps")
        oh_ready = [sem(f"onehot_ready{s}") for s in range(2)]
        oh_used = [sem(f"onehot_used{s}") for s in range(2)]
        slot_used = [sem(f"slot_used{s}") for s in range(2)]
        cnt_ready, tiles_ready, base_ready = sem("cnt_ready"), sem("tiles_ready"), sem("base_ready")
        reached_ready, blk_ready, blk_used = sem("reached_ready"), sem("blk_ready"), sem("blk_used")
        sorted_dst = sem("sorted_dst")
        staged = [sem(f"staged_dst{s}") for s in range(2)]
        sent = [sem(f"sent_dst{s}") for s in range(2)]
        var_ready, root_ready, h_ready, h_stored = sem("var0"), sem("root0"), sem("h0_ready"), sem("h0_stored")

        ZD, ZS = TILES * WD, TILES * WS

        with nc.Block() as block:
            @block.sync
            def _(sp):
                sp.dma_start(dst_i[:], dst_in.rearrange("(p c) -> p c", p=EP)).then_inc(idx_loaded, 16)
                sp.dma_start(src_i[:], src_in.rearrange("(p c) -> p c", p=EP)).then_inc(idx_loaded, 16)
                sp.dma_start(et_i[:], et_in.rearrange("(p c) -> p c", p=EP)).then_inc(et_loaded, 16)
                sp.dma_start(coeff[:].rearrange("p r b -> p (r b)"),
                             coeff_in.rearrange("r b -> (r b)").unsqueeze(0).to_broadcast([P, RELS * BASES])
                             ).then_inc(et_loaded, 16)
                sp.wait_ge(x_padded, 1)
                sp.dma_start(x[:, 0:NB - 1, :], x_in[0:(NB - 1) * P, :].rearrange("(b p) d -> p b d", p=P)).then_inc(x_loaded, 16)
                sp.dma_start(x[0:NT, NB - 1, :], x_in[(NB - 1) * P:N, :]).then_inc(x_loaded, 16)
                sp.wait_ge(zero_ready, 1)
                dst_flat = by_dst.rearrange("(p r) w -> p (r w)", p=P)
                src_flat = by_src.rearrange("(p r) w -> p (r w)", p=P)
                for table, size in ((dst_flat, ZD), (src_flat, ZS)):
                    for at in range(0, size, NB * D):
                        n = min(NB * D, size - at)
                        sp.dma_start(table[:, at:at + n], zero[:, 0:n]).then_inc(zeroed, 16)
                sp.wait_ge(h_ready, 1)
                sp.dma_start(h_tab.rearrange("(b p) d -> p b d", p=P), h[:]).then_inc(h_stored, 16)
                sp.wait_ge(h_stored, 16)

            @block.gpsimd
            def _(pool):
                ch = Chain(pool, built)

                def keep_where(ap, op, fill, base, pattern, mult=1):
                    ch.link(nc.gpsimd.affine_select(out=ap, in_=ap, compare_op=op, fill=fill, base=base,
                                                    pattern=pattern, channel_multiplier=mult))
                ch.link(nc.gpsimd.memset(ident[:], 0.0))
                keep_where(ident[:], ALU.not_equal, 1.0, 0, [[-1, P]])
                for table, size, base in ((place, P, 1), (minus, P, -1), (bins, NBIN, 0), (tile_no, TILES, 0)):
                    ch.link(nc.gpsimd.iota(table[:], pattern=[[1 if base >= 0 else -1, size]], base=base, channel_multiplier=0,
                                           allow_small_or_imprecise_dtypes=True))
                ch.link(nc.gpsimd.memset(before[:], 1.0))
                keep_where(before[:], ALU.is_gt, 0.0, 0, [[1, P]], -1)
                ch.link(nc.gpsimd.memset(lower[:], 1.0))
                for half in range(2):
                    keep_where(lower[:, 64 * half:64 * half + 64], ALU.is_gt, 0.0, 0, [[1, 64]], -1)
                ch.link(nc.gpsimd.memset(hilo[:], 0.0))
                keep_where(hilo[:], ALU.not_equal, 256.0, 0, [[-1, NBIN]])
                keep_where(hilo[:], ALU.not_equal, 1.0, -64, [[-1, NBIN]])
                ch.link(nc.gpsimd.memset(twice[:], 0.0))
                ch.link(nc.gpsimd.memset(twice[:, 128:129], 1.0))
                ch.link(nc.gpsimd.memset(twice[:, 192:193], 1.0))
                ch.link(nc.gpsimd.memset(real[:], 1.0))
                keep_where(real[:], ALU.is_ge, 0.0, -1, [[0, 1]])
                keep_where(real[:], ALU.is_ge, 0.0, NB - 1, [[0, 1]], -1)
                ch.link(nc.gpsimd.memset(eps[:], LN_EPS))
                ch.link(nc.gpsimd.memset(zeros16[:], 0.0))
                nc.gpsimd.memset(ones[:], 1.0).then_inc(consts, 1)
                pool.wait_ge(zeroed, 16 * (-(-ZD // (NB * D)) + -(-ZS // (NB * D))))
                scatter_pool(nc, pool, by_dst, rows, words, staged, sent)

            @block.scalar
            def _(act):
                act.wait_ge(sorted_dst, 1)

                def copies(i, s, at):
                    nc.scalar.activation(rows[:, s, :], row_dst[:, bass.ds(at, SC)], ACT.Copy)
                    nc.scalar.activation(words[:, s, :, 0:1], src_i[:, bass.ds(at, SC)].unsqueeze(2), ACT.Copy)
                    return nc.scalar.activation(words[:].bitcast(F32)[:, s, :, 1:WD], wordf[:, bass.ds(at, SC), :], ACT.Copy)
                norm_scalar(nc, act, stat, eps, var_ready, root_ready)
                stage_scalar(act, copies, staged, sent, 0, EC // (2 * SC))

            @block.vector
            def _(dve):
                ch = Chain(dve, steps)
                for s in range(2):
                    dve.nop(nofuse=True).then_inc(oh_used[s], 1)
                    dve.nop(nofuse=True).then_inc(slot_used[s], 1)
                nc.vector.memset(x[:, NB - 1, :], 0.0).then_inc(x_padded, 1)
                nc.vector.memset(zero, 0).then_inc(zero_ready, 1)
                dve.wait_ge(idx_loaded, 32)
                dve.wait_ge(consts, 1)
                nc.vector.tensor_copy(dstf[:], dst_i[:])

                def sort(turn, key, place_out, sign, row_out, blk):
                    ch.link(nc.vector.tensor_scalar(int_a[0:EP, :], key[:], 7, None, ALU.logical_shift_right))
                    ch.link(nc.vector.tensor_scalar(int_b[0:EP, :], key[:], P - 1, None, ALU.bitwise_and))
                    ch.link(nc.vector.tensor_copy(binf[:], int_a[0:EP, :]))
                    ch.link(nc.vector.tensor_scalar(place_out, int_b[0:EP, :].unsqueeze(2), 1.0, sign, ALU.add, ALU.mult))
                    half = NBIN // 2
                    with dve.Fori(0, half) as i:
                        for s in range(2):
                            dve.wait_ge(oh_used[s], i + (turn * 2 * half + 1))
                            nc.vector.tensor_scalar(onehot[s][:], binf[:], bins[0:EP, bass.ds(2 * i + s, 1)], None,
                                                    ALU.is_equal).then_inc(oh_ready[s], 1)
                    dve.wait_ge(cnt_ready, turn + 1)
                    ch.link(nc.vector.tensor_copy(cnt[:].rearrange("p (c q) -> p c q", c=4), banks[0][:, :, 0:CQ]))
                    ch.link(nc.vector.memset(int_b[:], 0))
                    ch.link(nc.vector.tensor_tensor_scan(run[:], cnt[:], int_b[:].bitcast(F32), 0.0, ALU.add, ALU.add))
                    ch.link(nc.vector.tensor_tensor(cnt[:], run[:], cnt[:], ALU.subtract))
                    ch.link(nc.vector.tensor_scalar(tint[:, 0:1], run[:, EC - 1:EC], float(P - 1), None, ALU.add))
                    ch.link(nc.vector.tensor_scalar(tint[:, 1:2], tint[:, 0:1], 7, None, ALU.logical_shift_right))
                    nc.vector.tensor_copy(tcol[:, 0:1], tint[:, 1:2]).then_inc(tiles_ready, 1)
                    dve.wait_ge(base_ready, turn + 1)
                    ch.link(nc.vector.tensor_copy(tcol[:, 1:2], banks[1][:, 0, 0:1]))
                    nc.vector.tensor_scalar(reached[:], tile_no[:], tcol[:, 1:2], None, ALU.is_ge).then_inc(reached_ready, 1)
                    ch.link(nc.vector.tensor_scalar(tcol[:, 2:3], tcol[:, 1:2], float(P), None, ALU.mult))
                    ch.link(nc.vector.tensor_scalar(int_a[:], cnt[:], tcol[:, 2:3], None, ALU.add))
                    ch.link(nc.vector.tensor_scalar(int_b[0:64, :], int_a[0:64, :], 8, None, ALU.logical_shift_right))
                    ch.link(nc.vector.tensor_scalar(int_b[64:P, :], int_a[64:P, :], 255, None, ALU.bitwise_and))
                    ch.link(nc.vector.tensor_copy(start[:], int_b[:]))
                    dve.wait_ge(blk_ready, turn + 1)
                    nc.vector.tensor_copy(blk[:].rearrange("p (c q) -> p c q", c=4), banks[1][0:1, :, 0:TILES // 4]).then_inc(blk_used, 1)
                    with dve.Fori(0, half) as i:
                        for s in range(2):
                            dve.wait_ge(slot_used[s], i + (turn * half + 1))
                            nc.vector.tensor_scalar(sel[s][:], ones[:, 0:EP], hilo[:, bass.ds(2 * i + s, 1)], None, ALU.mult)
                            nc.vector.tensor_scalar(onehot[s][:], binf[:], bins[0:EP, bass.ds(2 * i + s, 1)], None,
                                                    ALU.is_equal).then_inc(oh_ready[s], 1)
                        for s in range(2):
                            dve.wait_ge(oh_used[s], i + (turn * 2 * half + half + 2))
                            if s:
                                dve.wait_ge(slot_used[0], i + (turn * half + 2))
                            else:
                                dve.wait_ge(slot_used[1], i + (turn * half + 1))
                            dve.nop(nofuse=True)
                            nc.vector.copy_predicated(pos[0:EP, :].rearrange("p (c q) -> p c q", c=4),
                                                      onehot[s][:].bitcast(U16).rearrange("p (c q) -> p c q", c=4),
                                                      banks[s][0:EP, :, 0:CQ]).then_inc(slot_used[s], 1)
                    dve.wait_ge(slot_used[1], (turn + 1) * half + 1)
                    a, b = int_a[0:EP, :], int_b[0:EP, :]
                    c = int_p[0:EP, :]
                    ch.link(nc.vector.tensor_copy(c, pos[0:EP, :]))
                    ch.link(nc.vector.tensor_scalar(a, c, 10, 10, ALU.logical_shift_right, ALU.logical_shift_left))
                    ch.link(nc.vector.tensor_scalar(b, c, P - 1, 3, ALU.bitwise_and, ALU.logical_shift_left))
                    ch.link(nc.vector.tensor_tensor(a, a, b, ALU.bitwise_or))
                    ch.link(nc.vector.tensor_scalar(b, c, 7, G - 1, ALU.logical_shift_right, ALU.bitwise_and))
                    ch.link(nc.vector.tensor_tensor(row_out[:], a, b, ALU.bitwise_or))

                int_p = cnt[:].bitcast(I32)
                dve.wait_ge(et_loaded, 32)
                for b in range(BASES):
                    for r in range(RELS):
                        ch.link(nc.vector.tensor_scalar(is_rel, et_i[:], float(r), None, ALU.is_equal))
                        w = wordf[:, :, 1 + b]
                        if r == 0:
                            ch.link(nc.vector.tensor_scalar(w, is_rel, coeff[0:EP, r, b:b + 1], None, ALU.mult))
                        else:
                            ch.link(nc.vector.scalar_tensor_tensor(w, is_rel, coeff[0:EP, r, b:b + 1], w, ALU.mult, ALU.add))
                sort(0, dst_i, wordf[:, :, 0:1], 1.0, row_dst, blk_dst)
                nc.vector.memset(tcol[:, 0:1], 0.0).then_inc(sorted_dst, 1)
                dve.wait_ge(x_loaded, 32)
                dve.wait_ge(zeroed, 16 * (-(-ZD // (NB * D)) + -(-ZS // (NB * D))))
                norm_vector(nc, dve, ch, stat, x, h, tmp, var_ready, root_ready)
                nc.vector.memset(tcol[:, 0:1], 0.0).then_inc(h_ready, 1)
                sort(1, src_i, srcf[:].unsqueeze(2), -1.0, row_src, blk_src)

            @block.tensor
            def _(pe):
                pe.wait_ge(consts, 1)
                half = NBIN // 2
                for turn in range(2):
                    if turn:
                        pe.wait_ge(slot_used[1], turn * half + 1)
                        pe.wait_ge(slot_used[0], turn * half + 1)
                    for c in range(4):
                        nc.tensor.matmul(banks[0][:, c, 0:CQ], twice[:, 0:P], zeros16[:], start=True, stop=False)
                    with pe.Fori(0, half) as i:
                        for s in range(2):
                            pe.wait_ge(oh_ready[s], i + turn * 2 * half + 1)
                            pe.nop(nofuse=True)
                            for c in range(4):
                                last = nc.tensor.matmul(banks[0][:, c, 0:CQ], twice[0:EP, bass.ds((P - s) - i * 2, P)],
                                                        onehot[s][:, c * CQ:(c + 1) * CQ], start=False, stop=False)
                            last.then_inc(oh_used[s], 1)
                    for c in range(4):
                        last = nc.tensor.matmul(banks[0][:, c, 0:CQ], twice[:, 0:P], zeros16[:], start=False, stop=True)
                    last.then_inc(cnt_ready, 1)
                    pe.wait_ge(tiles_ready, turn + 1)
                    nc.tensor.matmul(banks[1][:, 0, 0:1], lower[:], tcol[:, 0:1], start=True, stop=True).then_inc(base_ready, 1)
                    pe.wait_ge(reached_ready, turn + 1)
                    for c in range(4):
                        last = nc.tensor.matmul(banks[1][0:1, c, 0:TILES // 4], real[:], reached[:, c * (TILES // 4):(c + 1) * (TILES // 4)],
                                                start=True, stop=True)
                    last.then_inc(blk_ready, 1)
                    pe.wait_ge(blk_used, turn + 1)
                    pe.nop(nofuse=True)
                    with pe.Fori(0, half) as i:
                        for s in range(2):
                            pe.wait_ge(oh_ready[s], i + turn * 2 * half + half + 1)
                            pe.wait_ge(slot_used[s], i + (turn * half + 1))
                            for c in range(4):
                                cut = slice(c * CQ, (c + 1) * CQ)
                                nc.tensor.matmul(banks[s][0:EP, c, 0:CQ], before[0:EP, 0:EP], onehot[s][:, cut], start=True, stop=False)
                                last = nc.tensor.matmul(banks[s][0:EP, c, 0:CQ], sel[s][:], start[:, cut], start=False, stop=True)
                            last.then_inc(oh_used[s], 1)


def load_group(sp, table, words, g, ready):
    rows = table.rearrange("(g r) w -> g (r w)", r=P * G)
    sp.dma_start(words[:].rearrange("p j w -> p (j w)"),
                 rows[bass.ds(g, 1), :].rearrange("a (p c) -> (a p) c", p=P)).then_inc(ready, 16)


def gather_group(pool, table, words, rows, width, ready):
    for j in range(G):
        pool.indirect_dma_start(rows[:, j, 0:width], None, table,
                                bass.IndirectOffsetOnAxis(ap=words[:, j, 0:1], axis=0)).then_inc(ready, 16)


def one_hot(nc, dve_out, place, places, tiles):
    return nc.vector.tensor_tensor(dve_out, place[:].unsqueeze(1).to_broadcast([P, tiles, P]),
                                   places.to_broadcast([P, tiles, P]), ALU.is_equal)


def upper(words):
    return words.bitcast(BF16).rearrange("... (c two) -> ... c two", two=2)[..., 1]


def sum_phase(nc, tag, acc, cols, place, blk, sorted_edges, width, table):
    T2 = 2 * G
    with ExitStack() as own:
        sb = lambda name, shape, dt=F32: own.enter_context(nc.sbuf_tensor(f"{tag}_{name}", list(shape), dt))
        sem = lambda name: own.enter_context(nc.semaphore(f"{tag}_{name}"))
        words = [sb(f"words{s}", [P, G, width], I32) for s in range(2)]
        rows = [sb(f"rows{s}", [P, G, cols]) for s in range(2)]
        onehot = [sb(f"onehot{s}", [P, G, P]) for s in range(2)]
        sums = [own.enter_context(nc.psum_tensor(f"{tag}_sums{s}", [P, G, GAP], F32)) for s in range(2)]
        words_ready = [sem(f"words_ready{s}") for s in range(2)]
        rows_ready = [sem(f"rows_ready{s}") for s in range(2)]
        oh_ready, summed, added = sem("onehot_ready"), sem("summed"), sem("added")
        at = 1 if width == WD else 2

        with nc.Block() as block:
            @block.sync
            def _(sp):
                with sp.Fori(0, ITERS) as i:
                    for s in range(2):
                        sp.wait_ge(summed, i * T2 + (s * G + G))
                        load_group(sp, sorted_edges, words[s], 2 * i + s, words_ready[s])

            @block.gpsimd
            def _(pool):
                with pool.Fori(0, ITERS) as i:
                    for s in range(2):
                        pool.wait_ge(words_ready[s], i * 16 + 16)
                        pool.wait_ge(summed, i * T2 + (s * G + G))
                        pool.nop(nofuse=True)
                        gather_group(pool, table, words[s], rows[s], D, rows_ready[s])

            @block.vector
            def _(dve):
                if cols > D:
                    for s in range(2):
                        nc.vector.memset(rows[s][:, :, D:cols], 1.0)
                nc.vector.memset(acc[:], 0.0).then_inc(added, T2)
                dve.nop(nofuse=True).then_inc(summed, T2)
                with dve.Fori(0, ITERS) as i:
                    for s in range(2):
                        dve.wait_ge(words_ready[s], i * 16 + 16)
                        one_hot(nc, onehot[s][:], place, words[s][:].bitcast(F32)[:, :, at:at + 1], G).then_inc(oh_ready, 1)
                        blocks = blocks_of(nc, ENGINE.DVE, blk, i * T2 + s * G, G)
                        for j in range(G):
                            if j % 2 == 0:
                                dve.wait_ge(summed, i * T2 + (s * G + j + 2 + T2))
                            dve.wait_ge(added, i * T2 + (s * G + j + T2))
                            a = acc[:, bass.ds(blocks[j], 1), :]
                            nc.vector.tensor_tensor(a, a, sums[s][:, j:j + 1, 0:cols], ALU.add).then_inc(added, 1)

            @block.tensor
            def _(pe):
                with pe.Fori(0, ITERS) as i:
                    for s in range(2):
                        pe.wait_ge(oh_ready, i * 2 + (s + 1))
                        pe.wait_ge(rows_ready[s], i * (16 * G) + 16 * G)
                        for j in range(G):
                            if j % 2 == 0:
                                pe.wait_ge(added, i * T2 + (s * G + j + 2))
                            nc.tensor.matmul(sums[s][:, j, 0:cols], onehot[s][:, j, :], rows[s][:, j, :],
                                             start=True, stop=True).then_inc(summed, 1)


def mean_phase(nc, acc, x, h, tmp, stat, ident, eps, wl_in, bl_in, wr_in, h_tab, edge, ea_in, by_src):
    dst_i, srcf, dstf, row_src = edge
    with ExitStack() as own:
        sb = lambda name, shape, dt=F32: own.enter_context(nc.sbuf_tensor(f"l0n_{name}", list(shape), dt))
        sem = lambda name: own.enter_context(nc.semaphore(f"l0n_{name}"))
        ps = lambda name: own.enter_context(nc.psum_tensor(f"l0n_{name}", [P, LB + 1, P], F32))
        w_raw = sb("w_raw", [P, 2, D])
        wT = sb("wT", [P, 2, D])
        bias = sb("bias", [P, D])
        a7, h7 = sb("a7", [P, LB, D]), sb("h7", [P, LB, D])
        aT, hT = sb("aT", [P, LB, P]), sb("hT", [P, LB, P])
        ps_a, ps_h, ps_o = ps("ps_a"), ps("ps_h"), ps("ps_o")
        rows = sb("rows", [EP, 2, SC], I32)
        attr = [sb(f"attr{s}", [EP, SC, ED]) for s in range(2)]
        words = sb("words", [EP, 2, SC, WS], I32)
        staged = [sem(f"staged{s}") for s in range(2)]
        sent = [sem(f"sent{s}") for s in range(2)]
        attr_ready = [sem(f"attr_ready{s}") for s in range(2)]
        w_loaded, wT_ready, wT_copied, steps = sem("w_loaded"), sem("wT_ready"), sem("wT_copied"), sem("steps")
        taken, turned, copied, product, summed = sem("taken"), sem("turned"), sem("copied"), sem("product"), sem("summed")
        var_ready, root_ready, h_ready, h_stored = sem("var"), sem("root"), sem("h_ready"), sem("h_stored")
        rounds = EC // (2 * SC)

        with nc.Block() as block:
            @block.sync
            def _(sp):
                sp.dma_start(w_raw[:, 0, :], wl_in).then_inc(w_loaded, 16)
                sp.dma_start(w_raw[:, 1, :], wr_in).then_inc(w_loaded, 16)
                sp.dma_start(bias[:], bl_in.unsqueeze(0).to_broadcast([P, D])).then_inc(w_loaded, 16)
                ea = ea_in.rearrange("(p c) w -> p (c w)", p=EP)
                for s in range(2):
                    sp.dma_start(attr[s][:].rearrange("p c w -> p (c w)"),
                                 ea[:, s * SC * ED:(s + 1) * SC * ED]).then_inc(attr_ready[s], 16)

                def attributes(i):
                    for s in range(2):
                        sp.wait_ge(staged[s], i)
                        sp.dma_start(attr[s][:].rearrange("p c w -> p (c w)"),
                                     ea[:, bass.ds(i * (2 * SC * ED) + s * SC * ED, SC * ED)]).then_inc(attr_ready[s], 16)
                with sp.Fori(1, rounds // 2) as i:
                    attributes(i)
                sp.wait_ge(h_ready, 1)
                sp.dma_start(h_tab.rearrange("(b p) d -> p b d", p=P), h[:]).then_inc(h_stored, 16)
                with sp.Fori(rounds // 2, rounds) as i:
                    attributes(i)
                sp.wait_ge(h_stored, 16)

            @block.gpsimd
            def _(pool):
                scatter_pool(nc, pool, by_src, rows, words, staged, sent)

            @block.scalar
            def _(act):
                wf = words[:].bitcast(F32)

                def copies(i, s, at):
                    act.wait_ge(attr_ready[s], i * 16 + 16)
                    nc.scalar.activation(rows[:, s, :], row_src[:, bass.ds(at, SC)], ACT.Copy)
                    nc.scalar.activation(words[:, s, :, 0:1], dst_i[:, bass.ds(at, SC)].unsqueeze(2), ACT.Copy)
                    nc.scalar.activation(wf[:, s, :, 1:2], dstf[:, bass.ds(at, SC)].unsqueeze(2), ACT.Copy)
                    nc.scalar.activation(wf[:, s, :, 2:3], srcf[:, bass.ds(at, SC)].unsqueeze(2), ACT.Copy)
                    return nc.scalar.activation(wf[:, s, :, 3:WS], attr[s][:], ACT.Copy)
                stage_scalar(act, copies, staged, sent, 0, rounds // 2)
                norm_scalar(nc, act, stat, eps, var_ready, root_ready)
                stage_scalar(act, copies, staged, sent, rounds // 2, rounds)

            @block.vector
            def _(dve):
                ch = Chain(dve, steps)
                ch.link(nc.vector.tensor_scalar(stat[:, 0, :].unsqueeze(2), acc[:, :, D:D + 1], 1.0, None, ALU.max))
                ch.link(nc.vector.reciprocal(stat[:, 1, :], stat[:, 0, :]))
                dve.nop(nofuse=True).then_inc(turned, 1)
                dve.wait_ge(wT_ready, 1)
                nc.vector.tensor_copy(wT[:], ps_o[:, 0:2, :]).then_inc(wT_copied, 1)
                dve.wait_ge(w_loaded, 48)
                ch.link(nc.vector.tensor_tensor(x[:], x[:], bias[:].unsqueeze(1).to_broadcast([P, NB, D]), ALU.add))
                with dve.Fori(0, NB // LB) as i:
                    here = bass.ds(i * LB, LB)
                    dve.wait_ge(turned, i + 1)
                    nc.vector.tensor_tensor(a7[:], acc[:, here, 0:D], stat[:, 1, here].unsqueeze(2).to_broadcast([P, LB, D]), ALU.mult)
                    nc.vector.tensor_copy(h7[:], h[:, here, :]).then_inc(taken, 1)
                    dve.wait_ge(turned, i + 2)
                    nc.vector.tensor_copy(aT[:], ps_a[:, 0:LB, :])
                    nc.vector.tensor_copy(hT[:], ps_h[:, 0:LB, :]).then_inc(copied, 1)
                    dve.wait_ge(product, i + 1)
                    nc.vector.tensor_tensor(x[:, here, :], x[:, here, :], ps_o[:, 0:LB, :], ALU.add).then_inc(summed, 1)
                dve.wait_ge(summed, NB // LB)
                norm_vector(nc, dve, ch, stat, x, h, tmp, var_ready, root_ready)
                nc.vector.memset(stat[:, 0, 0:1], 0.0).then_inc(h_ready, 1)

            @block.tensor
            def _(pe):
                pe.wait_ge(w_loaded, 48)
                for k in range(2):
                    last = nc.tensor.transpose(ps_o[:, k, :], w_raw[:, k, :], ident[:])
                last.then_inc(wT_ready, 1)
                pe.wait_ge(wT_copied, 1)
                pe.nop(nofuse=True)
                with pe.Fori(0, NB // LB) as i:
                    pe.wait_ge(taken, i + 1)
                    for src, dst in ((a7, ps_a), (h7, ps_h)):
                        for j in range(LB):
                            last = nc.tensor.transpose(dst[:, j, :], src[:, j, :], ident[:])
                    last.then_inc(turned, 1)
                    pe.wait_ge(copied, i + 1)
                    for j in range(LB):
                        nc.tensor.matmul(ps_o[:, j, :], aT[:, j, :], wT[:, 0, :], start=True, stop=False)
                        last = nc.tensor.matmul(ps_o[:, j, :], hT[:, j, :], wT[:, 1, :], start=False, stop=True)
                    last.then_inc(product, 1)


def relation_phase(nc, acc, place, minus, before, blk_dst, blk_src, by_dst, by_src, h_tab, rep):
    T2, H = 2 * G, G // 2
    with ExitStack() as own:
        sb = lambda name, shape, dt=F32: own.enter_context(nc.sbuf_tensor(f"l1_{name}", list(shape), dt))
        sem = lambda name: own.enter_context(nc.semaphore(f"l1_{name}"))
        ps = lambda name, shape: own.enter_context(nc.psum_tensor(f"l1_{name}", shape, F32))
        words_d = [sb(f"words_d{s}", [P, G, WD], I32) for s in range(2)]
        words_s = [sb(f"words_s{s}", [P, G, WS], I32) for s in range(2)]
        rows = [sb(f"rows{s}", [P, G, D]) for s in range(2)]
        msg = [sb(f"msg{s}", [P, G, 2 * D]) for s in range(2)]
        onehot = [sb(f"onehot{s}", [P, G, P]) for s in range(2)]
        apart = [sb(f"apart{q}", [P, H, P]) for q in range(2)]
        apart_ready = sem("apart_ready")
        onehot_s = [sb(f"onehot_s{s}", [P, G, P], BF16) for s in range(2)]
        rest = [sb(f"rest{n}", [P, G, WS - 1]) for n in range(2)]
        first = sb("first", [P, G, P], BF16)
        absent = sb("absent", [P, G, 1])
        sums = ps("sums", [P, G, GAP])
        rank = ps("rank", [P, G, P])
        pick = [ps(f"pick{s}", [P, G, 64]) for s in range(2)]
        split = sem("split")
        dready = [sem(f"words_d_ready{b}") for b in range(4)]
        sready = [sem(f"words_s_ready{s}") for s in range(2)]
        rows_ready = [sem(f"rows_ready{b}") for b in range(4)]
        scaled, summed, added, kept = sem("scaled"), sem("summed"), sem("added"), sem("kept")
        oh_ready, ohs_ready, ranked, firsts, picked, absent_ready = (
            sem("onehot_ready"), sem("onehot_s_ready"), sem("ranked"), sem("firsts"), sem("picked"), sem("absent_ready"))

        with nc.Block() as block:
            @block.sync
            def _(sp):
                table = by_dst.rearrange("(g r) w -> g (r w)", r=P * G)
                with sp.Fori(0, ITERS) as i:
                    for s in range(2):
                        for q in range(2):
                            sp.wait_ge(oh_ready, i * 4 + (2 * s + q + 1))
                            sp.nop(nofuse=True)
                            sp.wait_ge(scaled, i * T2 + (s * G + (q + 1) * H))
                            sp.dma_start(words_d[s][:, q * H:(q + 1) * H, :].rearrange("p j w -> p (j w)"),
                                         table[bass.ds(i * 2 + s, 1), :].rearrange("a (p c) -> (a p) c", p=P)[:, q * H * WD:(q + 1) * H * WD]
                                         ).then_inc(dready[2 * s + q], 16)
                        sp.wait_ge(picked, i * 2 + (s + 1))
                        load_group(sp, by_src, words_s[s], 2 * i + s, sready[s])

            @block.gpsimd
            def _(pool):
                with pool.Fori(0, ITERS) as i:
                    for b in range(4):
                        s, q = b // 2, b % 2
                        pool.wait_ge(dready[b], i * 16 + 16)
                        pool.wait_ge(scaled, i * T2 + (b + 1) * H)
                        pool.nop(nofuse=True)
                        for j in range(q * H, (q + 1) * H):
                            pool.indirect_dma_start(rows[s][:, j, :], None, h_tab,
                                                    bass.IndirectOffsetOnAxis(ap=words_d[s][:, j, 0:1], axis=0)).then_inc(rows_ready[b], 16)

            @block.scalar
            def _(act):
                def by_destination(i, s, q):
                    h = s % 2
                    act.wait_ge(dready[2 * h + q], i * 16 + (16 + 16 * (s // 2)))
                    act.wait_ge(oh_ready, i * 4 + (2 * s + q + 3))
                    for j in range(H):
                        last = nc.scalar.activation(apart[q][:, j, :], minus[:], ACT.Abs,
                                                    bias=words_d[h][:].bitcast(F32)[:, q * H + j, 1:2])
                    last.then_inc(apart_ready, 1)
                    act.wait_ge(apart_ready, i * 4 + (2 * s + q + 1))
                    act.wait_ge(summed, i * T2 + (s * G + (q + 1) * H))
                    nc.scalar.activation(onehot[h][:, q * H:(q + 1) * H, :], apart[q][:], ACT.Relu,
                                         bias=place[:, 0:1], scale=-1.0).then_inc(oh_ready, 1)

                def step(i, s, last=False):
                    for j in range(G):
                        if j % H == 0:
                            act.wait_ge(rows_ready[2 * s + j // H], i * (16 * H) + 16 * H)
                        if j % 2 == 0:
                            act.wait_ge(summed, i * T2 + (s * G + j + 2))
                        for b in range(BASES):
                            done = nc.scalar.activation(msg[s][:, j, b * D:(b + 1) * D], rows[s][:, j, :], ACT.Copy,
                                                        scale=words_d[s][:].bitcast(F32)[:, j, 2 + b:3 + b])
                        done.then_inc(scaled, 1)
                        if j % H == H - 1 and not last:
                            by_destination(i, s + 1, j // H)
                act.nop(nofuse=True).then_inc(oh_ready, 4)
                for q in range(2):
                    by_destination(0, 0, q)
                with act.Fori(0, ITERS - 1) as i:
                    for s in range(2):
                        step(i, s)
                step(ITERS - 1, 0)
                step(ITERS - 1, 1, last=True)

            @block.vector
            def _(dve):
                def by_source(i, s, q):
                    h, cut = s % 2, slice(q * H, (q + 1) * H)
                    if q == 0:
                        dve.wait_ge(sready[h], i * 16 + (16 + 16 * (s // 2)))
                    one_hot(nc, onehot_s[h][:, cut], minus, words_s[h][:].bitcast(F32)[:, cut, 2:3], H).then_inc(ohs_ready, 1)

                def split_words(i, s, n):
                    w = words_s[s % 2][:].bitcast(F32)[:, :, 1:WS] if n == 0 else rest[0][:]
                    dve.wait_ge(split, i * 4 + (2 * s + n + 1))
                    nc.vector.tensor_tensor(rest[n][:], w, upper(w), ALU.subtract).then_inc(split, 1)

                def first_edges(i, s, q):
                    cut = slice(q * H, (q + 1) * H)
                    dve.wait_ge(ranked, i * 4 + (2 * s + q + 1))
                    nc.vector.scalar_tensor_tensor(first[:, cut, :], rank[:, cut, :], 0.0, onehot_s[s % 2][:, cut, :],
                                                   ALU.is_equal, ALU.mult).then_inc(firsts, 1)

                def step(i, s, last=False):
                    blocks_d = blocks_of(nc, ENGINE.DVE, blk_dst, i * T2 + s * G, G)
                    blocks_s = blocks_of(nc, ENGINE.DVE, blk_src, i * T2 + s * G, G)
                    dve.wait_ge(picked, i * 2 + (s + 3))
                    dve.wait_ge(kept, i * T2 + (s * G + T2))
                    nc.vector.tensor_scalar(absent[:], pick[s][:, :, 1:2], 0.0, None, ALU.is_equal).then_inc(absent_ready, 1)
                    for j in range(G):
                        t = i * T2 + (s * G + j)
                        if j % 2 == 0:
                            dve.wait_ge(summed, t + (2 + T2))
                        dve.wait_ge(added, t + T2)
                        a = acc[:, bass.ds(blocks_d[j], 1), :]
                        nc.vector.tensor_tensor(a, a, sums[:, j:j + 1, :], ALU.add).then_inc(added, 1)
                        if j == 0:
                            dve.wait_ge(absent_ready, i * 2 + (s + 1))
                        dve.wait_ge(kept, t + T2)
                        r = rep[:, bass.ds(blocks_s[j], 1), :]
                        nc.vector.scalar_tensor_tensor(r, r, absent[:, j, :], pick[s][:, j:j + 1, 0:WS - 1], ALU.mult, ALU.add).then_inc(kept, 1)
                        if j == 0:
                            dve.wait_ge(firsts, i * 4 + (2 * s + 2))
                        if last:
                            continue
                        if j < 2:
                            by_source(i, s + 1, j)
                        if j in (2, 3):
                            split_words(i, s + 1, j - 2)
                        elif j in (4, 5):
                            first_edges(i, s + 1, j - 4)

                nc.vector.memset(rep[:], 0.0).then_inc(kept, T2)
                nc.vector.memset(acc[:], 0.0).then_inc(added, T2)
                dve.nop(nofuse=True).then_inc(scaled, T2)
                dve.nop(nofuse=True).then_inc(summed, T2)
                dve.nop(nofuse=True).then_inc(picked, 2)
                dve.nop(nofuse=True).then_inc(split, 1)
                for stage in (by_source, split_words, first_edges):
                    for q in range(2):
                        stage(0, 0, q)
                with dve.Fori(0, ITERS - 1) as i:
                    for s in range(2):
                        step(i, s)
                step(ITERS - 1, 0)
                step(ITERS - 1, 1, last=True)

            @block.tensor
            def _(pe):
                def ranks(i, s):
                    for j in range(G):
                        if j % H == 0:
                            pe.wait_ge(ohs_ready, i * 4 + (2 * s + j // H + 1))
                        if j == 0 and not (isinstance(i, int) and i == 0 and s == 0):
                            pe.wait_ge(firsts, i * 4 + 2 * s)
                        last = nc.tensor.matmul(rank[:, j, :], before[:], onehot_s[s % 2][:, j, :], start=True, stop=True)
                        if j % H == H - 1:
                            last.then_inc(ranked, 1)

                def picks(i, s):
                    for j in range(G):
                        if j % H == 0:
                            pe.wait_ge(firsts, i * 4 + (2 * s + j // H + 1))
                        if j == 0:
                            pe.wait_ge(split, i * 4 + (2 * s + 3))
                            pe.wait_ge(kept, i * T2 + (s * G + G))
                        parts = (words_s[s % 2][:].bitcast(F32)[:, j, 1:WS], rest[0][:, j, :], rest[1][:, j, :])
                        for n, w in enumerate(parts):
                            last = nc.tensor.matmul(pick[s % 2][:, j, 0:WS - 1], first[:, j, :], upper(w), start=(n == 0), stop=(n == 2))
                    last.then_inc(picked, 1)

                def step(i, s, last=False):
                    for j in range(G):
                        if j == H and not last:
                            ranks(i, s + 1)
                        if j % H == 0:
                            pe.wait_ge(oh_ready, i * 4 + (2 * s + j // H + 5))
                        if j % 2 == 0:
                            pe.wait_ge(added, i * T2 + (s * G + j + 2 + G))
                        pe.wait_ge(scaled, i * T2 + (s * G + j + 1 + T2))
                        nc.tensor.matmul(sums[:, j, :], onehot[s][:, j, :], msg[s][:, j, :], start=True, stop=True).then_inc(summed, 1)
                    if not last:
                        picks(i, s + 1)
                ranks(0, 0)
                picks(0, 0)
                with pe.Fori(0, ITERS - 1) as i:
                    for s in range(2):
                        step(i, s)
                step(ITERS - 1, 0)
                step(ITERS - 1, 1, last=True)


def project_phase(nc, acc, x, h, tmp, stat, ident, eps, w1_in, hb_in, loop_in, wq_in, bq_in, wk_in, bk_in,
                  wv_in, bv_in, we_in, wskip_in, bskip_in, kv_tab, qtab, skip):
    QS = D + QE + D
    with ExitStack() as own:
        sb = lambda name, shape, dt=F32: own.enter_context(nc.sbuf_tensor(f"l2p_{name}", list(shape), dt))
        sem = lambda name: own.enter_context(nc.semaphore(f"l2p_{name}"))
        w1 = sb("w1", [P, 4, D])
        bias1 = sb("bias1", [P, D])
        wqs = sb("wqs", [P, QS])
        wkv = sb("wkv", [P, 2 * D])
        bqs = sb("bqs", [P, QS])
        bkv = sb("bkv", [P, 2 * D])
        we = sb("we", [ED, D])
        bq_col = sb("bq_col", [P, 1])
        bq_wide = sb("bq_wide", [P, P])
        wqT, weT = sb("wqT", [P, P]), sb("weT", [P, ED])
        we_heads = sb("we_heads", [P, QE])
        room = qtab[:].rearrange("p b c -> p (b c)")
        in7, inT = (room[:, k * 3 * LB * D:(k + 1) * 3 * LB * D].rearrange("p (k b d) -> p k b d", k=3, b=LB) for k in range(2))
        h7, hT = sb("h7", [P, LB, D]), sb("hT", [P, LB, P])
        loaded, wT, wT_copied, wqe, ready = (sem(n) for n in ("loaded", "wT", "wT_copied", "wqe", "weights_ready"))
        steps, taken, turned, copied, product, summed = (sem(n) for n in ("steps", "taken", "turned", "copied", "product", "summed"))
        var_ready, root_ready, h_ready = sem("var"), sem("root"), sem("h_ready")
        taken2, turned2, copied2, qs_ready, kv_ready, qs_read, kv_read, kv_stored = (
            sem(n) for n in ("taken2", "turned2", "copied2", "qs_ready", "kv_ready", "qs_read", "kv_read", "kv_stored"))
        LOADS = 14
        R = NB // LB

        def first_half():
            with ExitStack() as mem:
                ps_i = [mem.enter_context(nc.psum_tensor(f"l2p_ps_i{k}", [P, LB + 1, P], F32)) for k in range(3)]
                ps_o = mem.enter_context(nc.psum_tensor("l2p_ps_o", [P, LB + 1, P], F32))
                with nc.Block() as block:
                    @block.sync
                    def _(sp):
                        def load(to, of):
                            sp.dma_start(to, of).then_inc(loaded, 16)
                        for k in range(3):
                            load(w1[:, k, :], w1_in[k])
                        load(w1[:, 3, :], loop_in)
                        load(bias1[:], hb_in.unsqueeze(0).to_broadcast([P, D]))
                        load(wqs[:, 0:D], wq_in)
                        load(wqs[:, D + QE:QS], wskip_in)
                        load(wkv[:, 0:D], wk_in)
                        load(wkv[:, D:2 * D], wv_in)
                        load(we[:], we_in)
                        load(bqs[:, 0:D], bq_in.unsqueeze(0).to_broadcast([P, D]))
                        load(bqs[:, D + QE:QS], bskip_in.unsqueeze(0).to_broadcast([P, D]))
                        load(bkv[:, 0:D], bk_in.unsqueeze(0).to_broadcast([P, D]))
                        load(bkv[:, D:2 * D], bv_in.unsqueeze(0).to_broadcast([P, D]))
                        load(bq_col[:], bq_in.unsqueeze(1))

                    @block.scalar
                    def _(act):
                        with act.Fori(0, R) as i:
                            here = bass.ds(i * LB, LB)
                            act.wait_ge(turned, i + 1)
                            nc.scalar.activation(in7[:, 0], h[:, here, :], ACT.Copy)
                            nc.scalar.activation(in7[:, 1], acc[:, here, 0:D], ACT.Copy)
                            nc.scalar.activation(in7[:, 2], acc[:, here, D:2 * D], ACT.Copy).then_inc(taken, 1)
                        norm_scalar(nc, act, stat, eps, var_ready, root_ready)

                    @block.vector
                    def _(dve):
                        ch = Chain(dve, steps)
                        dve.nop(nofuse=True).then_inc(turned, 1)
                        dve.wait_ge(loaded, 16 * (LOADS + 1))
                        ch.link(nc.vector.tensor_tensor(w1[:, 0, :], w1[:, 0, :], w1[:, 3, :], ALU.add))
                        ch.link(nc.vector.memset(we_heads[:], 0.0))
                        nc.vector.tensor_copy(bq_wide[:], bq_col[:].to_broadcast([P, P]))
                        dve.wait_ge(wT, 1)
                        nc.vector.tensor_copy(wqT[:], ps_o[:, 0, :])
                        for k in range(HEADS):
                            part = slice(k * HC, (k + 1) * HC)
                            last = nc.vector.tensor_copy(we_heads[part, k * ED:(k + 1) * ED], ps_o[part, 4, 0:ED])
                        last.then_inc(wT_copied, 1)
                        dve.wait_ge(wqe, 1)
                        nc.vector.tensor_copy(wqs[:, D:D + QE], ps_o[:, 0, 0:QE])
                        nc.vector.tensor_copy(bqs[:, D:D + QE], ps_o[:, 4, 0:QE]).then_inc(ready, 1)
                        ch.link(nc.vector.tensor_tensor(x[:], x[:], bias1[:].unsqueeze(1).to_broadcast([P, NB, D]), ALU.add))
                        with dve.Fori(0, R) as i:
                            here = bass.ds(i * LB, LB)
                            dve.wait_ge(turned, i + 2)
                            for k in range(3):
                                last = nc.vector.tensor_copy(inT[:, k], ps_i[k][:, 0:LB, :])
                            last.then_inc(copied, 1)
                            dve.wait_ge(product, i + 1)
                            nc.vector.tensor_tensor(x[:, here, :], x[:, here, :], ps_o[:, 0:LB, :], ALU.add).then_inc(summed, 1)
                        dve.wait_ge(summed, R)
                        norm_vector(nc, dve, ch, stat, x, h, tmp, var_ready, root_ready)

                    @block.tensor
                    def _(pe):
                        pe.wait_ge(loaded, 16 * (LOADS + 1))
                        nc.tensor.transpose(ps_o[:, 0, :], wqs[:, 0:D], ident[:])
                        nc.tensor.transpose(ps_o[:, 4, 0:ED], we[:], ident[0:ED, 0:ED]).then_inc(wT, 1)
                        pe.wait_ge(wT_copied, 1)
                        nc.tensor.matmul(ps_o[:, 0, 0:QE], wqT[:], we_heads[:], start=True, stop=True)
                        nc.tensor.matmul(ps_o[:, 4, 0:QE], bq_wide[:], we_heads[:], start=True, stop=True).then_inc(wqe, 1)
                        pe.wait_ge(ready, 1)
                        pe.nop(nofuse=True)
                        with pe.Fori(0, R) as i:
                            pe.wait_ge(taken, i + 1)
                            for k in range(3):
                                for j in range(LB):
                                    last = nc.tensor.transpose(ps_i[k][:, j, :], in7[:, k, j, :], ident[:])
                            last.then_inc(turned, 1)
                            pe.wait_ge(copied, i + 1)
                            for j in range(LB):
                                for k in range(3):
                                    last = nc.tensor.matmul(ps_o[:, j, :], inT[:, k, j, :], w1[:, k, :], start=(k == 0), stop=(k == 2))
                            last.then_inc(product, 1)

        def second_half():
            with ExitStack() as mem:
                ps_t = mem.enter_context(nc.psum_tensor("l2p_ps_t", [P, LB + 1, P], F32))
                ps_qs = [mem.enter_context(nc.psum_tensor(f"l2p_qs{k}", [P, 512], F32)) for k in range(3)]
                ps_kv = [mem.enter_context(nc.psum_tensor(f"l2p_kv{k}", [P, 512], F32)) for k in range(3)]
                with nc.Block() as block:
                    @block.sync
                    def _(sp):
                        rows = kv_tab.rearrange("(r b p) c -> r p b c", b=LB, p=P)
                        with sp.Fori(0, R) as i:
                            sp.wait_ge(kv_read, i * LB + (LB + 1))
                            sp.dma_start(rows[bass.ds(i, 1)].rearrange("a p b c -> (a p) b c"), acc[:, bass.ds(i * LB, LB), :]).then_inc(kv_stored, 16)
                        sp.wait_ge(kv_stored, 16 * R)

                    @block.scalar
                    def _(act):
                        for n in (turned2, kv_ready, kv_read):
                            act.nop(nofuse=True).then_inc(n, 1)
                        with act.Fori(0, R) as i:
                            act.wait_ge(turned2, i + 1)
                            nc.scalar.activation(h7[:], h[:, bass.ds(i * LB, LB), :], ACT.Copy).then_inc(taken2, 1)
                            act.wait_ge(turned2, i + 2)
                            act.wait_ge(kv_ready, i * LB + 1)
                            nc.scalar.activation(hT[:], ps_t[:, 0:LB, :], ACT.Copy).then_inc(copied2, 1)

                    @block.vector
                    def _(dve):
                        with dve.Fori(0, R) as i:
                            for j in range(LB):
                                b = bass.ds(i * LB + j, 1)
                                dve.wait_ge(qs_ready, i * LB + j + 1)
                                qs = ps_qs[j % 3][:].unsqueeze(1)
                                nc.vector.tensor_tensor(qtab[:, b, 0:D + QE], qs[:, :, 0:D + QE], bqs[:, 0:D + QE].unsqueeze(1), ALU.add)
                                nc.vector.tensor_tensor(skip[:, b, :], qs[:, :, D + QE:QS], bqs[:, D + QE:QS].unsqueeze(1), ALU.add).then_inc(qs_read, 1)
                                dve.wait_ge(kv_ready, i * LB + (j + 2))
                                nc.vector.tensor_tensor(acc[:, b, :], ps_kv[j % 3][:, 0:2 * D].unsqueeze(1), bkv[:].unsqueeze(1), ALU.add).then_inc(kv_read, 1)

                    @block.tensor
                    def _(pe):
                        with pe.Fori(0, R) as i:
                            pe.wait_ge(taken2, i + 1)
                            for j in range(LB):
                                last = nc.tensor.transpose(ps_t[:, j, :], h7[:, j, :], ident[:])
                            last.then_inc(turned2, 1)
                            pe.wait_ge(copied2, i + 1)
                            for j in range(LB):
                                if j < 3:
                                    pe.wait_ge(kv_read, i * LB + 1)
                                else:
                                    pe.wait_ge(kv_read, i * LB + (j - 1))
                                nc.tensor.matmul(ps_qs[j % 3][:, 0:QS], hT[:, j, :], wqs[:], start=True, stop=True).then_inc(qs_ready, 1)
                                nc.tensor.matmul(ps_kv[j % 3][:, 0:2 * D], hT[:, j, :], wkv[:], start=True, stop=True).then_inc(kv_ready, 1)

        first_half()
        second_half()


def attend_phase(nc, whole, acc, qtab, h, rep, ident, place, blk, by_src, kv_tab):
    T2, Q = 2 * G, G // 2
    SCALE = HC ** -0.5
    C = D + HEADS
    with ExitStack() as own:
        sb = lambda name, shape, dt=F32: own.enter_context(nc.sbuf_tensor(f"l2_{name}", list(shape), dt))
        sem = lambda name: own.enter_context(nc.semaphore(f"l2_{name}"))
        ps = lambda name, shape: own.enter_context(nc.psum_tensor(f"l2_{name}", shape, F32))
        words = [sb(f"words{s}", [P, G, WS], I32) for s in range(2)]
        kv = [sb(f"kv{s}", [P, G, 2 * D]) for s in range(2)]
        room, used = h[:].rearrange("p b d -> p (b d)"), [0]

        def carve(tiles, size):
            at = used[0]
            used[0] += tiles * size
            return room[:, at:at + tiles * size].rearrange("p (t c) -> p t c", t=tiles)
        onehot = [carve(G, P) for s in range(2)]
        apart = [carve(Q, P) for q in range(2)]
        turned = [carve(Q, P) for q in range(2)]
        msg = [carve(Q, C) for q in range(2)]
        prod = carve(Q, HEADS * (HC + ED)).rearrange("p t (n c) -> p t n c", n=HEADS)
        score = [sb(f"score{q}", [P, 2, Q, HEADS]) for q in range(2)]
        ps_t = [ps(f"ps_t{q}", [P, Q, P]) for q in range(2)]
        ps_q = [ps(f"ps_q{q}", [P, Q, GAP]) for q in range(2)]
        ps_s = ps("ps_s", [P, Q, GAP])
        idx = sb("idx", [P, NB, 1], I32)
        part = sb("part", [P, 2, NB, HEADS])
        one = sb("one", [P, 1])
        idx_ready, guard_rows, guard_steps, guard_ready = sem("idx_ready"), sem("guard_rows"), sem("guard_steps"), sem("guard_ready")
        words_ready = [sem(f"words_ready{b}") for b in range(4)]
        kv_ready = [sem(f"kv_ready{b}") for b in range(4)]
        names = ("onehot_ready", "flipped", "flip_copied", "queried", "multiplied", "scored", "exped", "msg_ready", "summed", "added", "steps", "apart_ready")
        oh_ready, flipped, flip_copied, queried, multiplied, scored, exped, msg_ready, summed, added, steps, apart_ready = (sem(n) for n in names)

        HALVES = 2 * GROUPS

        def half(m):
            return m // 2 % 2, m % 2

        def steps_of(eng, step):
            step(0, 0)
            rounds = (HALVES - 1) // 4
            with eng.Fori(0, rounds) as i:
                for n in range(1, 5):
                    step(i, n)
            for m in range(4 * rounds + 1, HALVES):
                step(rounds, m - 4 * rounds)

        def last_of(i, n, ahead):
            return isinstance(i, int) and 4 * i + n + ahead >= HALVES

        with nc.Block() as block:
            @block.sync
            def _(sp):
                rows = by_src.rearrange("(g r) w -> g (r w)", r=P * G)

                def load(i, b):
                    s, q = half(b)
                    sp.dma_start(words[s][:, q * Q:(q + 1) * Q, :].rearrange("p j w -> p (j w)"),
                                 rows[bass.ds(i * 2 + s, 1), :].rearrange("a (p c) -> (a p) c", p=P)[:, q * Q * WS:(q + 1) * Q * WS]
                                 ).then_inc(words_ready[b], 16)
                for b in range(4):
                    load(0, b)
                with sp.Fori(1, ITERS) as i:
                    for b in range(4):
                        sp.wait_ge(scored, i * 4 + (b - 3))
                        load(i, b)

            @block.gpsimd
            def _(pool):
                def gather(b):
                    s, q = half(b)
                    for e in range(q * Q, (q + 1) * Q):
                        pool.indirect_dma_start(kv[s][:, e, :], None, kv_tab, bass.IndirectOffsetOnAxis(ap=words[s][:, e, 0:1], axis=0)
                                                ).then_inc(kv_ready[b], 16)
                pool.wait_ge(idx_ready, 1)
                pool.nop(nofuse=True)
                for b in range(NB):
                    pool.indirect_dma_start(whole[:, b, :], None, kv_tab, bass.IndirectOffsetOnAxis(ap=idx[:, b, :], axis=0)
                                            ).then_inc(guard_rows, 16)
                for b in range(4):
                    pool.wait_ge(words_ready[b], 16)
                    pool.nop(nofuse=True)
                    gather(b)
                with pool.Fori(1, ITERS) as i:
                    for b in range(4):
                        pool.wait_ge(words_ready[b], i * 16 + 16)
                        pool.wait_ge(msg_ready, i * 4 + (b - 3))
                        pool.nop(nofuse=True)
                        gather(b)

            @block.scalar
            def _(act):
                def flip_copy(i, n):
                    act.wait_ge(flipped, 4 * i + (n + 1))
                    nc.scalar.activation(turned[n % 2], ps_t[n % 2][:], ACT.Copy).then_inc(flip_copied, 1)

                def one_hots(i, n):
                    s, q = half(n)
                    cut = slice(q * Q, (q + 1) * Q)
                    act.wait_ge(words_ready[n % 4], (i + n // 4) * 16 + 16)
                    if not (isinstance(i, int) and 4 * i + n < 2):
                        act.wait_ge(oh_ready, 4 * i + (n - 1))
                    for e in range(Q):
                        last = nc.scalar.activation(apart[q][:, e, :], place[:], ACT.Abs, bias=words[s][:].bitcast(F32)[:, q * Q + e, 2:3])
                    last.then_inc(apart_ready, 1)
                    act.wait_ge(apart_ready, 4 * i + (n + 1))
                    nc.scalar.activation(onehot[s][:, cut, :], apart[q], ACT.Relu, bias=one[:, 0:1], scale=-1.0).then_inc(oh_ready, 1)

                def step(i, n):
                    if not last_of(i, n, 1):
                        flip_copy(i, n + 1)
                    q = n % 2
                    act.wait_ge(scored, 4 * i + (n + 1))
                    nc.scalar.activation(msg[q][:, :, D:C], score[q][:, 1], ACT.Exp, scale=SCALE).then_inc(exped, 1)
                    if not last_of(i, n, 2):
                        one_hots(i, n + 2)
                act.wait_ge(guard_ready, 1)
                one_hots(0, 0)
                one_hots(0, 1)
                flip_copy(0, 0)
                steps_of(act, step)

            @block.vector
            def _(dve):
                ch = Chain(dve, guard_steps)
                nc.vector.memset(one[:], 1.0)
                nc.vector.tensor_copy(idx[:], rep[:, :, 0:1]).then_inc(idx_ready, 1)
                by_head = h[:, :, 0:QE].rearrange("p b (n e) -> p b n e", n=HEADS)
                for k in range(HEADS):
                    last = nc.vector.tensor_tensor(by_head[:, :, k, :], qtab[:, :, D + k * ED:D + (k + 1) * ED], rep[:, :, 2:WS - 1], ALU.mult)
                ch.link(last)
                ch.link(nc.vector.tensor_reduce(part[:, 0], by_head, AX.X, ALU.add))
                dve.wait_ge(guard_rows, 16 * NB)
                ch.link(nc.vector.tensor_tensor(h[:], qtab[:, :, 0:D], whole[:, :, 0:D], ALU.mult))
                ch.link(nc.vector.tensor_reduce(part[:, 1], h[:].rearrange("p b (n c) -> p b n c", n=HEADS), AX.X, ALU.add))
                nc.vector.tensor_tensor(qtab[:, :, D + QE:QW], part[:, 0], part[:, 1], ALU.add).then_inc(guard_ready, 1)
                nc.vector.memset(acc, 0.0).then_inc(added, G)

                def add(i, n, e, blocks):
                    if e % 2 == 0:
                        dve.wait_ge(summed, i * T2 + (n * Q + e + 2))
                    dve.wait_ge(added, i * T2 + (n * Q + e + G))
                    a = acc[:, bass.ds(blocks[e], 1), :]
                    nc.vector.tensor_tensor(a, a, ps_s[:, e:e + 1, 0:C], ALU.add).then_inc(added, 1)

                def step(i, n):
                    s, q = half(n)
                    cut = slice(q * Q, (q + 1) * Q)
                    first = isinstance(i, int) and 4 * i + n == 0
                    heads = lambda ap, c: ap.rearrange("p t (n c) -> p t n c", n=HEADS)
                    blocks = None if first else blocks_of(nc, ENGINE.DVE, blk, i * T2 + (n - 1) * Q, Q)

                    def add_before(e):
                        if not first:
                            add(i, n - 1, e, blocks)
                    sc = score[q]
                    dve.wait_ge(queried, 4 * i + (n + 1))
                    dve.wait_ge(kv_ready[n % 4], (i + n // 4) * (16 * Q) + 16 * Q)
                    nc.vector.tensor_tensor(prod[:, :, :, 0:HC], heads(ps_q[q][:, :, 0:D], HC), heads(kv[s][:, cut, 0:D], HC), ALU.mult)
                    add_before(0)
                    nc.vector.tensor_tensor(prod[:, :, :, HC:HC + ED], heads(ps_q[q][:, :, D:D + QE], ED),
                                            words[s][:].bitcast(F32)[:, cut, 3:WS].unsqueeze(2).to_broadcast([P, Q, HEADS, ED]),
                                            ALU.mult).then_inc(multiplied, 1)
                    add_before(1)
                    dve.wait_ge(multiplied, 4 * i + (n + 1))
                    nc.vector.tensor_reduce(sc[:, 0], prod, AX.X, ALU.add).then_inc(steps, 1)
                    add_before(2)
                    dve.wait_ge(steps, 4 * i + (n + 1))
                    nc.vector.tensor_tensor(sc[:, 1], sc[:, 0], ps_q[q][:, :, D + QE:QW], ALU.subtract).then_inc(scored, 1)
                    add_before(3)
                    dve.wait_ge(exped, 4 * i + (n + 1))
                    nc.vector.tensor_tensor(heads(msg[q][:, :, 0:D], HC), heads(kv[s][:, cut, D:2 * D], HC),
                                            msg[q][:, :, D:C].unsqueeze(3).to_broadcast([P, Q, HEADS, HC]),
                                            ALU.mult).then_inc(msg_ready, 1)
                steps_of(dve, step)
                blocks = blocks_of(nc, ENGINE.DVE, blk, TILES - Q, Q)
                for e in range(Q):
                    add(0, HALVES - 1, e, blocks)

            @block.tensor
            def _(pe):
                def flip(i, n):
                    s, q = half(n)
                    pe.wait_ge(oh_ready, 4 * i + (n + 1))
                    for e in range(Q):
                        last = nc.tensor.transpose(ps_t[q][:, e, :], onehot[s][:, q * Q + e, :], ident[:])
                    last.then_inc(flipped, 1)

                def sum_up(i, n):
                    s, q = half(n)
                    pe.wait_ge(msg_ready, 4 * i + (n + 1))
                    for e in range(Q):
                        nc.tensor.matmul(ps_s[:, e, 0:C], onehot[s][:, q * Q + e, :], msg[q][:, e, :], start=True, stop=True).then_inc(summed, 1)

                def step(i, n):
                    q = n % 2
                    blocks = blocks_of(nc, ENGINE.PE, blk, i * T2 + n * Q, Q)
                    pe.wait_ge(flip_copied, 4 * i + (n + 1))
                    for e in range(Q):
                        last = nc.tensor.matmul(ps_q[q][:, e, 0:QW], turned[q][:, e, :],
                                                qtab[:, bass.ds(blocks[e], 1), :].rearrange("p a c -> p (a c)"), start=True, stop=True)
                    last.then_inc(queried, 1)
                    if not (isinstance(i, int) and 4 * i + n == 0):
                        sum_up(i, n - 1)
                    if not last_of(i, n, 1):
                        flip(i, n + 1)
                pe.wait_ge(guard_ready, 1)
                flip(0, 0)
                steps_of(pe, step)
                sum_up(0, HALVES - 1)


def beta_phase(nc, acc, skip, x, h, tmp, stat, eps, wbeta_in, h_tab):
    with ExitStack() as own:
        sb = lambda name, shape, dt=F32: own.enter_context(nc.sbuf_tensor(f"l2b_{name}", list(shape), dt))
        sem = lambda name: own.enter_context(nc.semaphore(f"l2b_{name}"))
        wb = sb("wb", [P, 3, D])
        wz = sb("wz", [P, 2, D])
        rden = sb("rden", [P, NB, HEADS])
        z = sb("z", [P, 4, NB])
        loaded, steps, z_ready, e_ready = sem("loaded"), sem("steps"), sem("z_ready"), sem("exp_ready")
        var_ready, root_ready, h_ready, h_stored = sem("var"), sem("root"), sem("h_ready"), sem("h_stored")
        att = h
        with nc.Block() as block:
            @block.sync
            def _(sp):
                sp.dma_start(wb[:].rearrange("p k d -> p (k d)"),
                             wbeta_in.rearrange("k o -> (k o)").unsqueeze(0).to_broadcast([P, 3 * D])).then_inc(loaded, 16)
                sp.wait_ge(h_ready, 1)
                sp.dma_start(h_tab.rearrange("(b p) d -> p b d", p=P), h[:]).then_inc(h_stored, 16)
                sp.wait_ge(h_stored, 16)

            @block.scalar
            def _(act):
                act.wait_ge(z_ready, 1)
                nc.scalar.activation(z[:, 1, :], z[:, 0, :], ACT.Exp, scale=-1.0).then_inc(e_ready, 1)
                norm_scalar(nc, act, stat, eps, var_ready, root_ready)

            @block.vector
            def _(dve):
                ch = Chain(dve, steps)
                ch.link(nc.vector.tensor_scalar(rden[:], acc[:, :, D:D + HEADS], 1e-16, None, ALU.add))
                ch.link(nc.vector.reciprocal(rden[:], rden[:]))
                for k in range(HEADS):
                    part = slice(k * HC, (k + 1) * HC)
                    last = nc.vector.tensor_tensor(att[:, :, part], acc[:, :, part], rden[:, :, k:k + 1].to_broadcast([P, NB, HC]), ALU.mult)
                ch.link(last)
                dve.wait_ge(loaded, 16)
                nc.vector.tensor_tensor(wz[:, 0, :], wb[:, 0, :], wb[:, 2, :], ALU.add)
                ch.link(nc.vector.tensor_tensor(wz[:, 1, :], wb[:, 1, :], wb[:, 2, :], ALU.subtract))
                for k, part in enumerate((att, skip)):
                    ch.link(nc.vector.tensor_tensor(tmp[:], part[:], wz[:, k, :].unsqueeze(1).to_broadcast([P, NB, D]), ALU.mult))
                    ch.link(nc.vector.tensor_reduce(z[:, 2 + k, :], tmp[:], AX.X, ALU.add))
                nc.vector.tensor_tensor(z[:, 0, :], z[:, 2, :], z[:, 3, :], ALU.add).then_inc(z_ready, 1)
                ch.link(nc.vector.tensor_tensor(skip[:], skip[:], att[:], ALU.subtract))
                ch.link(nc.vector.tensor_tensor(x[:], x[:], att[:], ALU.add))
                dve.wait_ge(e_ready, 1)
                ch.link(nc.vector.tensor_scalar(z[:, 2, :], z[:, 1, :], 1.0, None, ALU.add))
                ch.link(nc.vector.reciprocal(z[:, 3, :], z[:, 2, :]))
                ch.link(nc.vector.tensor_tensor(skip[:], skip[:], wide(z[:, 3, :]), ALU.mult))
                ch.link(nc.vector.tensor_tensor(x[:], x[:], skip[:], ALU.add))
                norm_vector(nc, dve, ch, stat, x, h, tmp, var_ready, root_ready)
                nc.vector.memset(z[:, 0, 0:1], 0.0).then_inc(h_ready, 1)


def final_phase(nc, acc, x, out):
    with nc.semaphore("last_sum") as done, nc.semaphore("out_stored") as stored:
        with nc.Block() as block:
            @block.vector
            def _(dve):
                nc.vector.tensor_tensor(x[:], x[:], acc, ALU.add).then_inc(done, 1)

            @block.sync
            def _(sp):
                sp.wait_ge(done, 1)
                sp.dma_start(out[0:(NB - 1) * P, :].rearrange("(b p) d -> p b d", p=P), x[:, 0:NB - 1, :]).then_inc(stored, 16)
                sp.dma_start(out[(NB - 1) * P:N, :], x[0:NT, NB - 1, :]).then_inc(stored, 16)
                sp.wait_ge(stored, 32)


_INS = ["x", "src", "dst", "edge_attr_16", "edge_type_8", "L0_gnn_W_l", "L0_gnn_b_l", "L0_gnn_W_r", "L1_gnn_coeff",
        "L1_gnn_W", "L1_gnn_h_bias", "L1_gnn_loop_weight", "L2_gnn_Wq", "L2_gnn_bq", "L2_gnn_Wk", "L2_gnn_bk",
        "L2_gnn_Wv", "L2_gnn_bv", "L2_gnn_We", "L2_gnn_Wskip", "L2_gnn_bskip", "L2_gnn_Wbeta"]


def kernel(**inputs):
    import numpy as _np
    import concourse.bacc as _bacc
    from concourse import mybir as _mybir
    from concourse.bass_utils import run_bass_kernel_spmd as _run

    nc = _bacc.Bacc("TRN2", target_bir_lowering=False, num_devices=1)
    arrays, args = {}, []
    for name in _INS:
        a = _np.ascontiguousarray(inputs[name])
        arrays[f"in_{name}"] = a
        args.append(nc.dram_tensor(f"in_{name}", a.shape, _mybir.dt.from_np(a.dtype), kind="ExternalInput").ap())
    args.append(nc.dram_tensor("out_x", (N, D), _mybir.dt.float32, kind="ExternalOutput").ap())
    build(nc, *args)
    r = _run(nc, [arrays], core_ids=[0])
    return r.results[0]["out_x"]
```
